# Optimizing a Trainium2 kernel written in Bass

```python
import numpy as np
import jax
import jax.numpy as jnp

def _softmax(x, axis=-1):
    return jax.nn.softmax(x, axis=axis)

def _gelu(x):
    return jax.nn.gelu(x, approximate=True)

def _silu(x):
    return jax.nn.silu(x)

def _sigmoid(x):
    return jax.nn.sigmoid(x)

def _layernorm(x, axis=-1, eps=1e-05):
    m = jnp.mean(x, axis=axis, keepdims=True)
    v = jnp.var(x, axis=axis, keepdims=True)
    return (x - m) / jnp.sqrt(v + eps)

def _scatter_add(tgt, idx, src, axis=0):
    return tgt.at[idx].add(src)

def _segment_sum(src, seg, n):
    return jax.ops.segment_sum(src, seg, n)
kernel_name = 'mk_decoder_postln_d2_seqx_r4_4818c7'

def setup_inputs(seed: int=0):
    np.random.seed(seed)
    _w = jnp.asarray

    def _rec_inputs():
        import jax
        import jax.numpy as jnp
        _rk = jax.random.key(seed)
        x = -0.0002928 + 1 * jax.random.normal(jax.random.fold_in(_rk, 1), (32, 128, 256), jnp.float32)
        _lenS = 128 - jax.random.randint(jax.random.fold_in(_rk, 7), (32,), 0, max(1, 128 // 4) + 1, jnp.int32)
        _lenS2 = 128 - jax.random.randint(jax.random.fold_in(_rk, 8), (32,), 0, max(1, 128 // 4) + 1, jnp.int32)
        _ctx_1024P = jax.random.normal(jax.random.fold_in(_rk, 11), (32, 16, 256), jnp.float32)
        _ctx_1024c = jax.random.dirichlet(jax.random.fold_in(_rk, 511), 0.3 * jnp.ones((16,), jnp.float32), (32, 128))
        _ctx_1024t = jnp.einsum('bsk,bkd->bsd', _ctx_1024c, _ctx_1024P)
        _ctx_1024t = _ctx_1024t * jax.lax.rsqrt(jnp.mean(jnp.square(_ctx_1024t)) + 1e-12) * 0.953939
        ctx_1024 = -1.39393e-06 + 0.999914 * (_ctx_1024t + 0.3 * jax.random.normal(jax.random.fold_in(_rk, 611), (32, 128, 256), jnp.float32))
        return (x, ctx_1024)
    x, ctx_1024 = _rec_inputs()

    def _L0_attn_setup():
        import jax, jax.numpy as jnp
        import numpy as np
        B, T, D = (1, 512, 256)
        H = 16
        HD = D // H
        WINDOW = 128
        NEG = -10000000000.0

        def _mask(t):
            i = jnp.arange(t)[:, None]
            j = jnp.arange(t)[None, :]
            return ((j <= i) & (j >= i - WINDOW)).astype(jnp.float32)

        def _genetic_fitness(g):
            t = g.shape[2]
            dot = jnp.einsum('bhid,bhjd->bhij', g, g)
            nrm = jnp.linalg.norm(g, axis=-1)
            corr = dot / (nrm[..., :, None] * nrm[..., None, :] + 1e-08)
            corr = jnp.nan_to_num(corr, nan=0.0, posinf=1.0, neginf=-1.0)
            m = _mask(t)[None, None]
            corr = corr * m
            corr = (corr + 1.0) / 2.0
            gene_means = jnp.mean(corr, axis=3)
            denom = gene_means + 0.5
            sum_inv = jnp.sum(1.0 / denom, axis=2, keepdims=True)
            gene_fitness = 1.0 / (denom * sum_inv)
            weighted = corr * gene_fitness[..., None]
            masked = weighted * m + (1.0 - m) * NEG
            return jax.nn.softmax(masked, axis=-1)
        key = jax.random.key(seed)
        ks = jax.random.split(key, 7)
        s = 1.0 / np.sqrt(D)
        return {'x': jax.random.normal(ks[0], (B, T, D), jnp.float32), 'Wg': jax.random.normal(ks[1], (D, D), jnp.float32) * s, 'bg': jax.random.normal(ks[2], (D,), jnp.float32) * 0.01, 'Wv': jax.random.normal(ks[3], (D, D), jnp.float32) * s, 'bv': jax.random.normal(ks[4], (D,), jnp.float32) * 0.01, 'Wo': jax.random.normal(ks[5], (D, D), jnp.float32) * s, 'bo': jax.random.normal(ks[6], (D,), jnp.float32) * 0.01}
    _L0_attn_all = _L0_attn_setup()
    _L0_attn_in = {k: v for k, v in _L0_attn_all.items() if k in ('Wg', 'bg', 'Wv', 'bv', 'Wo', 'bo')}
    del _L0_attn_all

    def _L0_xattn_setup():
        import jax, jax.numpy as jnp
        import numpy as np
        D_MODEL = 256
        N_HEADS = 16
        D_HEAD = D_MODEL // N_HEADS
        WINDOW = 128

        def _heads(x):
            B, S, _ = x.shape
            return x.reshape(B, S, N_HEADS, D_HEAD).transpose(0, 2, 1, 3)
        key = jax.random.key(seed)
        ks = jax.random.split(key, 11)
        B, S = (1, 1024)
        s = 1.0 / np.sqrt(D_MODEL)
        return {'query': jax.random.normal(ks[0], (B, S, D_MODEL), jnp.float32), 'key': jax.random.normal(ks[1], (B, S, D_MODEL), jnp.float32), 'value': jax.random.normal(ks[2], (B, S, D_MODEL), jnp.float32), 'Wq': jax.random.normal(ks[3], (D_MODEL, D_MODEL), jnp.float32) * s, 'bq': jnp.zeros((D_MODEL,), jnp.float32), 'Wk': jax.random.normal(ks[4], (D_MODEL, D_MODEL), jnp.float32) * s, 'bk': jnp.zeros((D_MODEL,), jnp.float32), 'Wv': jax.random.normal(ks[5], (D_MODEL, D_MODEL), jnp.float32) * s, 'bv': jnp.zeros((D_MODEL,), jnp.float32), 'Wo': jax.random.normal(ks[6], (D_MODEL, D_MODEL), jnp.float32) * s, 'bo': jnp.zeros((D_MODEL,), jnp.float32)}
    _L0_xattn_all = _L0_xattn_setup()
    _L0_xattn_in = {k: v for k, v in _L0_xattn_all.items() if k in ('Wq', 'bq', 'Wk', 'bk', 'Wv', 'bv', 'Wo', 'bo')}
    del _L0_xattn_all

    def _L0_ffn_setup():
        import jax, jax.numpy as jnp
        import numpy as np
        EPS_RMS = 1e-06
        EPS_ACT = 1e-05

        def simple_rms_norm(x):
            ms = jnp.mean(jnp.square(x), axis=-1, keepdims=True)
            return x * jax.lax.rsqrt(ms + EPS_RMS)

        def activation_quant(x):
            absmax = jnp.max(jnp.abs(jax.lax.stop_gradient(x)), axis=-1, keepdims=True)
            scale = 127.0 / jnp.clip(absmax, EPS_ACT, None)
            q = jnp.clip(jnp.round(x * scale), -128.0, 127.0) / scale
            return x + jax.lax.stop_gradient(q - x)
        key = jax.random.key(seed)
        k1, k2, k3 = jax.random.split(key, 3)
        B, S, D_IN, D_OUT = (8, 2048, 256, 256)
        x = jax.random.normal(k1, (B, S, D_IN), dtype=jnp.float32)
        w_int8 = jax.random.randint(k2, (D_OUT, D_IN), -128, 128, dtype=jnp.int32)
        weight_scale = jnp.float32(127.0 / 0.06)
        bias = jax.random.normal(k3, (D_OUT,), dtype=jnp.float32) * 0.01
        return {'x': x, 'w_int8': w_int8, 'weight_scale': weight_scale, 'bias': bias}
    _L0_ffn_all = _L0_ffn_setup()
    _L0_ffn_in = {k: v for k, v in _L0_ffn_all.items() if k in ('w_int8', 'weight_scale', 'bias')}
    del _L0_ffn_all

    def _L1_attn_setup():
        import math
        import jax, jax.numpy as jnp
        import numpy as np
        L, B, D = (512, 8, 256)
        Z, H, N = (128, 512, 16)

        def _rotary_bias(rb_alpha, rb_beta, seq_len, z):
            half = z // 2
            freqs = jnp.exp(jnp.arange(half, dtype=jnp.float32) * (-math.log(10000.0) / half))
            pos = jnp.arange(seq_len, dtype=jnp.float32)[:, None] * freqs[None, :]
            sin, cos = (jnp.sin(pos), jnp.cos(pos))

            def rot(w):
                we = jnp.broadcast_to(w, (seq_len, z))
                w1, w2 = (we[:, :half], we[:, half:])
                return jnp.concatenate([w1 * cos - w2 * sin, w2 * cos + w1 * sin], axis=1)
            return rot(rb_alpha) @ rot(rb_beta).T

        def _ema(xn, ema_delta, ema_alpha, ema_beta, ema_gamma, ema_omega):
            seq_len = xn.shape[0]
            p = jax.nn.sigmoid(ema_delta)
            a = jax.nn.sigmoid(ema_alpha)
            q = 1.0 - p * a
            t = jnp.arange(seq_len, dtype=jnp.float32)[None, None, :]
            kern = p * ema_beta * jnp.exp(t * jnp.log(q))
            scale = math.sqrt(1.0 / kern.shape[1])
            k_dl = jnp.einsum('dnl,dn->dl', kern, ema_gamma * scale)
            xt = jnp.transpose(xn, (1, 2, 0))
            nfft = 2 * seq_len
            kf = jnp.fft.rfft(k_dl, n=nfft)
            xf = jnp.fft.rfft(xt, n=nfft)
            conv = jnp.fft.irfft(xf * kf, n=nfft)[..., :seq_len]
            return jax.nn.silu(jnp.transpose(conv, (2, 0, 1)) + xn * ema_omega)
        key = jax.random.key(seed)
        ks = jax.random.split(key, 16)
        s = 0.02
        inp = {'x': jax.random.normal(ks[0], (L, B, D), jnp.float32), 'ln_w': jnp.ones((D,), jnp.float32), 'ln_b': jnp.zeros((D,), jnp.float32), 'v_w': jax.random.normal(ks[1], (H, D), jnp.float32) * s, 'v_b': jnp.zeros((H,), jnp.float32), 'mx_w': jax.random.normal(ks[2], (Z + H + 2 * D, D), jnp.float32) * s, 'mx_b': jnp.zeros((Z + H + 2 * D,), jnp.float32), 'h_w': jax.random.normal(ks[3], (D, H), jnp.float32) * s, 'h_b': jnp.zeros((D,), jnp.float32), 'qk_gamma': jnp.ones((2, Z), jnp.float32) + jax.random.normal(ks[4], (2, Z), jnp.float32) * s, 'qk_beta': jax.random.normal(ks[5], (2, Z), jnp.float32) * s, 'ema_delta': jax.random.normal(ks[6], (D, N, 1), jnp.float32), 'ema_alpha': jax.random.normal(ks[7], (D, N, 1), jnp.float32), 'ema_beta': jax.random.normal(ks[8], (D, N, 1), jnp.float32) * s, 'ema_gamma': jax.random.normal(ks[9], (D, N), jnp.float32) * s, 'ema_omega': jax.random.normal(ks[10], (D,), jnp.float32) * s, 'rb_alpha': jax.random.normal(ks[11], (1, Z), jnp.float32) * s, 'rb_beta': jax.random.normal(ks[12], (1, Z), jnp.float32) * s}
        return inp
    _L1_attn_all = _L1_attn_setup()
    _L1_attn_in = {k: v for k, v in _L1_attn_all.items() if k in ('ln_w', 'ln_b', 'v_w', 'v_b', 'mx_w', 'mx_b', 'h_w', 'h_b', 'qk_gamma', 'qk_beta', 'ema_delta', 'ema_alpha', 'ema_beta', 'ema_gamma', 'ema_omega', 'rb_alpha', 'rb_beta')}
    del _L1_attn_all

    def _L1_xattn_setup():
        import jax, jax.numpy as jnp
        import numpy as np
        N, L, E, H, D = (4, 512, 256, 16, 64)
        key = jax.random.key(seed)
        ks = jax.random.split(key, 8)
        s = 1.0 / np.sqrt(E)
        return {'Q': jax.random.normal(ks[0], (N, L, E), jnp.float32), 'K': jax.random.normal(ks[1], (N, L, E), jnp.float32), 'V': jax.random.normal(ks[2], (N, L, E), jnp.float32), 'Wq': jax.random.normal(ks[3], (H * D, E), jnp.float32) * s, 'bq': jnp.zeros((H * D,), jnp.float32), 'Wk': jax.random.normal(ks[4], (H * D, E), jnp.float32) * s, 'bk': jnp.zeros((H * D,), jnp.float32), 'Wv': jax.random.normal(ks[5], (H * D, E), jnp.float32) * s, 'bv': jnp.zeros((H * D,), jnp.float32), 'Wo': jax.random.normal(ks[6], (E, H * D), jnp.float32) * s, 'bo': jnp.zeros((E,), jnp.float32)}
    _L1_xattn_all = _L1_xattn_setup()
    _L1_xattn_in = {k: v for k, v in _L1_xattn_all.items() if k in ('Wq', 'bq', 'Wk', 'bk', 'Wv', 'bv', 'Wo', 'bo')}
    del _L1_xattn_all

    def _L1_ffn_setup():
        import jax, jax.numpy as jnp
        import numpy as np
        HID, FFN, E, K = (256, 1024, 8, 2)
        CAP_FACTOR = 1.25
        key = jax.random.key(seed)
        k1, k2, k3, k4 = jax.random.split(key, 4)
        B, T = (4, 512)
        x = jax.random.normal(k1, (B, T, HID), dtype=jnp.float32)
        router_w = jax.random.normal(k2, (E, HID), dtype=jnp.float32) * 0.02
        w1 = jax.random.normal(k3, (E, HID, FFN), dtype=jnp.float32) * 0.02
        w2 = jax.random.normal(k4, (E, FFN, HID), dtype=jnp.float32) * 0.02
        return {'x': x, 'router_w': router_w, 'w1': w1, 'w2': w2}
    _L1_ffn_all = _L1_ffn_setup()
    _L1_ffn_in = {k: v for k, v in _L1_ffn_all.items() if k in ('router_w', 'w1', 'w2')}
    del _L1_ffn_all
    return {'x': x, 'ctx_1024': ctx_1024, 'L0_attn_Wg': _L0_attn_in['Wg'], 'L0_attn_bg': _L0_attn_in['bg'], 'L0_attn_Wv': _L0_attn_in['Wv'], 'L0_attn_bv': _L0_attn_in['bv'], 'L0_attn_Wo': _L0_attn_in['Wo'], 'L0_attn_bo': _L0_attn_in['bo'], 'L0_xattn_Wq': _L0_xattn_in['Wq'], 'L0_xattn_bq': _L0_xattn_in['bq'], 'L0_xattn_Wk': _L0_xattn_in['Wk'], 'L0_xattn_bk': _L0_xattn_in['bk'], 'L0_xattn_Wv': _L0_xattn_in['Wv'], 'L0_xattn_bv': _L0_xattn_in['bv'], 'L0_xattn_Wo': _L0_xattn_in['Wo'], 'L0_xattn_bo': _L0_xattn_in['bo'], 'L0_ffn_w_int8': _L0_ffn_in['w_int8'], 'L0_ffn_weight_scale': _L0_ffn_in['weight_scale'], 'L0_ffn_bias': _L0_ffn_in['bias'], 'L1_attn_ln_w': _L1_attn_in['ln_w'], 'L1_attn_ln_b': _L1_attn_in['ln_b'], 'L1_attn_v_w': _L1_attn_in['v_w'], 'L1_attn_v_b': _L1_attn_in['v_b'], 'L1_attn_mx_w': _L1_attn_in['mx_w'], 'L1_attn_mx_b': _L1_attn_in['mx_b'], 'L1_attn_h_w': _L1_attn_in['h_w'], 'L1_attn_h_b': _L1_attn_in['h_b'], 'L1_attn_qk_gamma': _L1_attn_in['qk_gamma'], 'L1_attn_qk_beta': _L1_attn_in['qk_beta'], 'L1_attn_ema_delta': _L1_attn_in['ema_delta'], 'L1_attn_ema_alpha': _L1_attn_in['ema_alpha'], 'L1_attn_ema_beta': _L1_attn_in['ema_beta'], 'L1_attn_ema_gamma': _L1_attn_in['ema_gamma'], 'L1_attn_ema_omega': _L1_attn_in['ema_omega'], 'L1_attn_rb_alpha': _L1_attn_in['rb_alpha'], 'L1_attn_rb_beta': _L1_attn_in['rb_beta'], 'L1_xattn_Wq': _L1_xattn_in['Wq'], 'L1_xattn_bq': _L1_xattn_in['bq'], 'L1_xattn_Wk': _L1_xattn_in['Wk'], 'L1_xattn_bk': _L1_xattn_in['bk'], 'L1_xattn_Wv': _L1_xattn_in['Wv'], 'L1_xattn_bv': _L1_xattn_in['bv'], 'L1_xattn_Wo': _L1_xattn_in['Wo'], 'L1_xattn_bo': _L1_xattn_in['bo'], 'L1_ffn_router_w': _L1_ffn_in['router_w'], 'L1_ffn_w1': _L1_ffn_in['w1'], 'L1_ffn_w2': _L1_ffn_in['w2']}

def reference(x, ctx_1024, L0_attn_Wg, L0_attn_bg, L0_attn_Wv, L0_attn_bv, L0_attn_Wo, L0_attn_bo, L0_xattn_Wq, L0_xattn_bq, L0_xattn_Wk, L0_xattn_bk, L0_xattn_Wv, L0_xattn_bv, L0_xattn_Wo, L0_xattn_bo, L0_ffn_w_int8, L0_ffn_weight_scale, L0_ffn_bias, L1_attn_ln_w, L1_attn_ln_b, L1_attn_v_w, L1_attn_v_b, L1_attn_mx_w, L1_attn_mx_b, L1_attn_h_w, L1_attn_h_b, L1_attn_qk_gamma, L1_attn_qk_beta, L1_attn_ema_delta, L1_attn_ema_alpha, L1_attn_ema_beta, L1_attn_ema_gamma, L1_attn_ema_omega, L1_attn_rb_alpha, L1_attn_rb_beta, L1_xattn_Wq, L1_xattn_bq, L1_xattn_Wk, L1_xattn_bk, L1_xattn_Wv, L1_xattn_bv, L1_xattn_Wo, L1_xattn_bo, L1_ffn_router_w, L1_ffn_w1, L1_ffn_w2):
    import jax
    import jax.numpy as jnp

    def _L0_attn_ref(x, Wg, bg, Wv, bv, Wo, bo):
        import jax, jax.numpy as jnp
        import numpy as np
        B, T, D = (1, 512, 256)
        H = 16
        HD = D // H
        WINDOW = 128
        NEG = -10000000000.0

        def _mask(t):
            i = jnp.arange(t)[:, None]
            j = jnp.arange(t)[None, :]
            return ((j <= i) & (j >= i - WINDOW)).astype(jnp.float32)

        def _genetic_fitness(g):
            t = g.shape[2]
            dot = jnp.einsum('bhid,bhjd->bhij', g, g)
            nrm = jnp.linalg.norm(g, axis=-1)
            corr = dot / (nrm[..., :, None] * nrm[..., None, :] + 1e-08)
            corr = jnp.nan_to_num(corr, nan=0.0, posinf=1.0, neginf=-1.0)
            m = _mask(t)[None, None]
            corr = corr * m
            corr = (corr + 1.0) / 2.0
            gene_means = jnp.mean(corr, axis=3)
            denom = gene_means + 0.5
            sum_inv = jnp.sum(1.0 / denom, axis=2, keepdims=True)
            gene_fitness = 1.0 / (denom * sum_inv)
            weighted = corr * gene_fitness[..., None]
            masked = weighted * m + (1.0 - m) * NEG
            return jax.nn.softmax(masked, axis=-1)
        b, t, d = x.shape
        g = x @ Wg.T + bg
        v = x @ Wv.T + bv
        g = g.reshape(b, t, H, HD).transpose(0, 2, 1, 3)
        v = v.reshape(b, t, H, HD).transpose(0, 2, 1, 3)
        attn = _genetic_fitness(g)
        out = jnp.einsum('bhij,bhjd->bhid', attn, v)
        out = out.transpose(0, 2, 1, 3).reshape(b, t, d)
        return out @ Wo.T + bo

    def _L0_xattn_ref(query, key, value, Wq, bq, Wk, bk, Wv, bv, Wo, bo):
        import jax, jax.numpy as jnp
        import numpy as np
        D_MODEL = 256
        N_HEADS = 16
        D_HEAD = D_MODEL // N_HEADS
        WINDOW = 128

        def _heads(x):
            B, S, _ = x.shape
            return x.reshape(B, S, N_HEADS, D_HEAD).transpose(0, 2, 1, 3)
        B, S, _ = query.shape
        q = _heads(query @ Wq.T + bq)
        k = _heads(key @ Wk.T + bk)
        v = _heads(value @ Wv.T + bv)
        scores = jnp.einsum('bhqd,bhkd->bhqk', q, k) / np.sqrt(D_HEAD).astype(np.float32)
        idx = jnp.arange(S)
        local = jnp.abs(idx[:, None] - idx[None, :]) <= WINDOW // 2
        scores = jnp.where(local[None, None, :, :], scores, -jnp.inf)
        attn = jax.nn.softmax(scores, axis=-1)
        ctx = jnp.einsum('bhqk,bhkd->bhqd', attn, v)
        ctx = ctx.transpose(0, 2, 1, 3).reshape(B, S, D_MODEL)
        return ctx @ Wo.T + bo

    def _L0_ffn_ref(x, w_int8, weight_scale, bias):
        import jax, jax.numpy as jnp
        import numpy as np
        EPS_RMS = 1e-06
        EPS_ACT = 1e-05

        def simple_rms_norm(x):
            ms = jnp.mean(jnp.square(x), axis=-1, keepdims=True)
            return x * jax.lax.rsqrt(ms + EPS_RMS)

        def activation_quant(x):
            absmax = jnp.max(jnp.abs(jax.lax.stop_gradient(x)), axis=-1, keepdims=True)
            scale = 127.0 / jnp.clip(absmax, EPS_ACT, None)
            q = jnp.clip(jnp.round(x * scale), -128.0, 127.0) / scale
            return x + jax.lax.stop_gradient(q - x)
        w_deq = w_int8.astype(jnp.float32) * (1.0 / weight_scale) * weight_scale ** 0 * weight_scale
        w_deq = w_int8.astype(jnp.float32) * weight_scale
        x_norm = simple_rms_norm(x)
        x_q = activation_quant(x_norm)
        return jnp.einsum('bsd,od->bso', x_q, w_deq) + bias

    def _L1_attn_ref(x, ln_w, ln_b, v_w, v_b, mx_w, mx_b, h_w, h_b, qk_gamma, qk_beta, ema_delta, ema_alpha, ema_beta, ema_gamma, ema_omega, rb_alpha, rb_beta):
        import math
        import jax, jax.numpy as jnp
        import numpy as np
        L, B, D = (512, 8, 256)
        Z, H, N = (128, 512, 16)

        def _rotary_bias(rb_alpha, rb_beta, seq_len, z):
            half = z // 2
            freqs = jnp.exp(jnp.arange(half, dtype=jnp.float32) * (-math.log(10000.0) / half))
            pos = jnp.arange(seq_len, dtype=jnp.float32)[:, None] * freqs[None, :]
            sin, cos = (jnp.sin(pos), jnp.cos(pos))

            def rot(w):
                we = jnp.broadcast_to(w, (seq_len, z))
                w1, w2 = (we[:, :half], we[:, half:])
                return jnp.concatenate([w1 * cos - w2 * sin, w2 * cos + w1 * sin], axis=1)
            return rot(rb_alpha) @ rot(rb_beta).T

        def _ema(xn, ema_delta, ema_alpha, ema_beta, ema_gamma, ema_omega):
            seq_len = xn.shape[0]
            p = jax.nn.sigmoid(ema_delta)
            a = jax.nn.sigmoid(ema_alpha)
            q = 1.0 - p * a
            t = jnp.arange(seq_len, dtype=jnp.float32)[None, None, :]
            kern = p * ema_beta * jnp.exp(t * jnp.log(q))
            scale = math.sqrt(1.0 / kern.shape[1])
            k_dl = jnp.einsum('dnl,dn->dl', kern, ema_gamma * scale)
            xt = jnp.transpose(xn, (1, 2, 0))
            nfft = 2 * seq_len
            kf = jnp.fft.rfft(k_dl, n=nfft)
            xf = jnp.fft.rfft(xt, n=nfft)
            conv = jnp.fft.irfft(xf * kf, n=nfft)[..., :seq_len]
            return jax.nn.silu(jnp.transpose(conv, (2, 0, 1)) + xn * ema_omega)
        seq_len, bsz, d = x.shape
        residual = x
        mu = jnp.mean(x, axis=-1, keepdims=True)
        var = jnp.mean(jnp.square(x - mu), axis=-1, keepdims=True)
        xn = (x - mu) * jax.lax.rsqrt(var + 1e-05) * ln_w + ln_b
        v = jax.nn.silu(xn @ v_w.T + v_b)
        mx = _ema(xn, ema_delta, ema_alpha, ema_beta, ema_gamma, ema_omega)
        base = mx @ mx_w.T + mx_b
        u = jax.nn.sigmoid(base[..., :d])
        zr = jax.nn.silu(base[..., d:d + Z + H])
        hx = base[..., d + Z + H:]
        z, r = (zr[..., :Z], zr[..., Z:])
        z2 = z[:, :, None, :] * qk_gamma + qk_beta
        q = jnp.transpose(z2[:, :, 0], (1, 0, 2)) * Z ** (-0.5)
        k = jnp.transpose(z2[:, :, 1], (1, 0, 2))
        vb = jnp.transpose(v, (1, 0, 2))
        bias = _rotary_bias(rb_alpha, rb_beta, seq_len, Z)
        attn = jax.nn.softmax(jnp.einsum('blz,bmz->blm', q, k) + bias, axis=-1)
        h = jnp.transpose(jnp.einsum('blm,bmh->blh', attn, vb), (1, 0, 2))
        h = jax.nn.silu(hx + h * r @ h_w.T + h_b)
        return residual + u * (h - residual)

    def _L1_xattn_ref(Q, K, V, Wq, bq, Wk, bk, Wv, bv, Wo, bo):
        import jax, jax.numpy as jnp
        import numpy as np
        N, L, E, H, D = (4, 512, 256, 16, 64)
        n, lq, e = Q.shape
        lk = K.shape[1]
        q = (Q @ Wq.T + bq).reshape(n, lq, H, D)
        k = (K @ Wk.T + bk).reshape(n, lk, H, D)
        v = (V @ Wv.T + bv).reshape(n, lk, H, D)
        scores = jnp.einsum('nqhd,nkhd->nqkh', q, k) / jnp.sqrt(jnp.float32(D))
        attn = jax.nn.softmax(scores, axis=2)
        out = jnp.einsum('nqkh,nkhd->nqhd', attn, v)
        out = out.reshape(n, lq, H * D)
        return (out @ Wo.T + bo).reshape(n, lq, E)

    def _L1_ffn_ref(x, router_w, w1, w2):
        import jax, jax.numpy as jnp
        import numpy as np
        HID, FFN, E, K = (256, 1024, 8, 2)
        CAP_FACTOR = 1.25
        B, T, H = x.shape
        N = B * T
        x_flat = x.reshape(N, H)
        C = max(1, int(CAP_FACTOR * N / E * K))
        logits = x_flat @ router_w.T
        probs = jax.nn.softmax(logits, axis=-1)
        top_v, top_i = jax.lax.top_k(probs, K)
        top_v = top_v / jnp.sum(top_v, axis=-1, keepdims=True)
        out = jnp.zeros_like(x_flat)
        for k in range(K):
            eid = top_i[:, k]
            gate = top_v[:, k]
            onehot = jax.nn.one_hot(eid, E, dtype=jnp.int32)
            pos = jnp.take_along_axis(jnp.cumsum(onehot, axis=0), eid[:, None], axis=1)[:, 0] - 1
            keep = pos < C
            slot = jnp.where(keep, eid * C + pos, E * C)
            buf = jnp.zeros((E * C + 1, H), dtype=x.dtype).at[slot].add(x_flat * keep[:, None].astype(x.dtype))
            expert_in = buf[:E * C].reshape(E, C, H)
            h = jax.nn.gelu(jnp.einsum('ech,ehf->ecf', expert_in, w1), approximate=False)
            y = jnp.einsum('ecf,efh->ech', h, w2)
            tok = y.reshape(E * C, H)[jnp.minimum(slot, E * C - 1)]
            out = out + tok * (gate * keep.astype(x.dtype))[:, None]
        return out.reshape(B, T, H)
    x = _layernorm(x + _L0_attn_ref(x, L0_attn_Wg, L0_attn_bg, L0_attn_Wv, L0_attn_bv, L0_attn_Wo, L0_attn_bo), axis=-1)
    x = _layernorm(x + _L0_xattn_ref(x, ctx_1024, ctx_1024, L0_xattn_Wq, L0_xattn_bq, L0_xattn_Wk, L0_xattn_bk, L0_xattn_Wv, L0_xattn_bv, L0_xattn_Wo, L0_xattn_bo), axis=-1)
    x = _layernorm(x + _L0_ffn_ref(x, L0_ffn_w_int8, L0_ffn_weight_scale, L0_ffn_bias), axis=-1)
    x = _layernorm(x + _L1_attn_ref(x, L1_attn_ln_w, L1_attn_ln_b, L1_attn_v_w, L1_attn_v_b, L1_attn_mx_w, L1_attn_mx_b, L1_attn_h_w, L1_attn_h_b, L1_attn_qk_gamma, L1_attn_qk_beta, L1_attn_ema_delta, L1_attn_ema_alpha, L1_attn_ema_beta, L1_attn_ema_gamma, L1_attn_ema_omega, L1_attn_rb_alpha, L1_attn_rb_beta), axis=-1)
    x = _layernorm(x + _L1_xattn_ref(x, ctx_1024, ctx_1024, L1_xattn_Wq, L1_xattn_bq, L1_xattn_Wk, L1_xattn_bk, L1_xattn_Wv, L1_xattn_bv, L1_xattn_Wo, L1_xattn_bo), axis=-1)
    x = _layernorm(x + _L1_ffn_ref(x, L1_ffn_router_w, L1_ffn_w1, L1_ffn_w2), axis=-1)
    return x

_drawn_inputs = setup_inputs


def setup_inputs(seed=0):
    import zlib

    import numpy as np

    out = dict(_drawn_inputs(seed))
    spreads = {'L0_xattn_bq': (0.0, 0.1),
     'L0_xattn_bk': (0.0, 0.1),
     'L0_xattn_bv': (0.0, 0.1),
     'L0_xattn_bo': (0.0, 0.1),
     'L1_attn_ln_w': (1.0, 0.2),
     'L1_attn_ln_b': (0.0, 0.1),
     'L1_attn_v_b': (0.0, 0.1),
     'L1_attn_mx_b': (0.0, 0.1),
     'L1_attn_h_b': (0.0, 0.1),
     'L1_xattn_bq': (0.0, 0.1),
     'L1_xattn_bk': (0.0, 0.1),
     'L1_xattn_bv': (0.0, 0.1),
     'L1_xattn_bo': (0.0, 0.1)}
    factors = {}
    for name, (base, spread) in spreads.items():
        noise = np.random.default_rng([zlib.crc32(name.encode()), seed]).standard_normal(out[name].shape)
        drawn = base * np.exp(spread * noise) if base else spread * noise
        out[name] = jnp.asarray(drawn.astype(out[name].dtype))
    for name, factor in factors.items():
        out[name] = (out[name] * factor).astype(out[name].dtype)
    return out
```

```python
import math
from contextlib import ExitStack

import numpy as np
import concourse.bass as bass
from concourse import mybir

F32 = mybir.dt.float32
BF16 = mybir.dt.bfloat16
I32 = mybir.dt.int32
U32 = mybir.dt.uint32
ALU = mybir.AluOpType
ACT = mybir.ActivationFunctionType
AX = mybir.AxisListType

P = 128
B, S, D = 32, 128, 256
TILES = B * S // P
H = 16
HALF = H // 2
HD = D // H
LN_EPS = 1e-5


def pipeline(eng, rounds, unroll, steps, depth=2):
    last_lag = max(lag for lag, _ in steps)

    def one_round(k, fixed):
        for u in range(unroll):
            for lag, f in steps:
                q = (u - lag) // unroll
                if not fixed or 0 <= k + q < rounds:
                    f(k + q, (u - lag) % unroll)

    head = -(-(last_lag + depth) // unroll)
    for k in range(min(head, rounds)):
        one_round(k, True)
    if head < rounds:
        with eng.Fori(head, rounds) as k:
            one_round(k, False)
    for k in range(rounds, rounds + -(-last_lag // unroll)):
        one_round(k, True)


def item_done(eng, sem, n, inc=1):
    eng.wait_ge(sem, (n + 1) * inc)


def slot_free(eng, sem, n, depth, inc=1):
    if type(n) is int and n < depth:
        return
    eng.wait_ge(sem, (n + (1 - depth)) * inc)


class Kit:

    def __init__(self, nc, stack, name):
        self.nc, self.stack, self.name, self.sems = nc, stack, name, []

    def sb(self, name, shape, dt=F32):
        return self.stack.enter_context(self.nc.sbuf_tensor(f"{self.name}_{name}", shape, dt))

    def ps(self, name, shape, dt=F32):
        return self.stack.enter_context(self.nc.psum_tensor(f"{self.name}_{name}", shape, dt))

    def sem(self, name):
        handle = self.stack.enter_context(self.nc.semaphore(f"{self.name}_{name}"))
        self.sems.append(handle.num)
        return handle

    def clear_semaphores(self):
        nums = sorted(self.sems)
        firsts = [n for n in nums if n - 1 not in nums]
        lasts = [n for n in nums if n + 1 not in nums]

        with self.nc.Block() as block:
            @block.sync
            def _(sp):
                for first, last in zip(firsts, lasts):
                    sp.sem_clear(range(first, last + 1))


def bcast(row, n=P):
    return row.partition_broadcast(n)


def spread(col, n):
    return col.unsqueeze(2).to_broadcast([col.shape[0], col.shape[1], n])


def per_tile(f):
    return lambda k, u: f(2 * k + u // 2, u // 2) if u % 2 == 0 else None


def per_unit(f):
    return lambda k, u: f(4 * k + u, 2 * k + u // 2, u // 2, u % 2)


def identity_f32(nc, pool, t, made):
    pool.memset(t[:, :], 0.0).then_inc(made, 1)
    pool.wait_ge(made, 1)
    pool.affine_select(out=t[:, :], in_=t[:, :], compare_op=ALU.not_equal, fill=1.0, base=0,
                       pattern=[[-1, P]], channel_multiplier=1).then_inc(made, 1)


def l0_attn(nc, x_in, wgv, bgv, att_out):
    with ExitStack() as stack:
        kit = Kit(nc, stack, "l0a")
        gv = kit.sb("gv", [P, TILES, D])
        va = kit.sb("va", [P, TILES, H, HD + 1])
        n2 = kit.sb("n2", [P, TILES, H])
        rn = kit.sb("rn", [P, TILES, H])
        ln = kit.sb("ln", [P, TILES, H])
        ident = kit.sb("ident", [P, P])
        l0_attn_project(nc, x_in, wgv, bgv, gv, va, n2, rn, ln, ident)
        l0_attn_heads(nc, gv, va, rn, ln, ident, att_out)


def l0_attn_project(nc, x_in, wgv, bgv, gv, va, n2, rn, ln, ident):
    with ExitStack() as stack:
        kit = Kit(nc, stack, "l0ap")
        w = kit.sb("w", [P, 2, 2 * D])
        bias = kit.sb("bias", [P, 2 * D])
        x = kit.sb("x", [P, 2, D])
        xt = kit.sb("xt", [P, 2, D])
        sq = kit.sb("sq", [P, 2, D])
        inv = kit.sb("inv", [P, TILES, H])
        lo = kit.sb("lo", [P, TILES, H])
        ps_t = [kit.ps(f"ps_t{u}", [P, D]) for u in range(2)]
        ps_gv = [kit.ps(f"ps_gv{u}", [P, 2 * D]) for u in range(2)]
        w_loaded, b_loaded, made = kit.sem("w_loaded"), kit.sem("b_loaded"), kit.sem("ident_made")
        x_loaded = [kit.sem(f"x_loaded{u}") for u in range(2)]
        xt_ready, xt_copied, gv_ready = kit.sem("xt_ready"), kit.sem("xt_copied"), kit.sem("gv_ready")
        g_biased, v_biased = kit.sem("g_biased"), kit.sem("v_biased")
        squared, summed, ones_set = kit.sem("squared"), kit.sem("summed"), kit.sem("ones_set")
        floored, clamped, rooted, logged = (kit.sem(n) for n in ("floored", "clamped", "rooted", "logged"))

        with nc.Block() as block:
            @block.sync
            def _(sp):
                sp.dma_start(w[:, :, :], wgv.rearrange("(k p) n -> p k n", p=P)).then_inc(w_loaded, 16)
                sp.dma_start(bias[:, :], bcast(bgv)).then_inc(b_loaded, 16)

                def load(k, u):
                    slot_free(sp, xt_ready, 2 * k + u, 2)
                    sp.dma_start(x[:, u, :], x_in[2 * k + u, :, :]).then_inc(x_loaded[u], 16)
                pipeline(sp, TILES // 2, 2, [(0, load)])

            @block.tensor
            def _(pe):
                pe.wait_ge(made, 2)

                def transposes(k, u):
                    n = 2 * k + u
                    item_done(pe, x_loaded[u], k, 16)
                    slot_free(pe, xt_copied, n, 2)
                    for c in range(2):
                        last = pe.transpose(ps_t[u][:, c * P:(c + 1) * P], x[:, u, c * P:(c + 1) * P], ident[:, :])
                    last.then_inc(xt_ready, 1)

                def project(k, u):
                    n = 2 * k + u
                    if type(n) is int and n == 0:
                        pe.wait_ge(w_loaded, 16)
                    item_done(pe, xt_copied, n)
                    slot_free(pe, v_biased, n, 2)
                    for c in range(2):
                        last = pe.matmul(ps_gv[u][:, :], xt[:, u, c * P:(c + 1) * P], w[:, c, :],
                                         start=c == 0, stop=c == 1)
                    last.then_inc(gv_ready, 1)
                pipeline(pe, TILES // 2, 2, [(0, transposes), (1, project)])

            @block.scalar
            def _(act):
                def copy_xt(k, u):
                    n = 2 * k + u
                    item_done(act, xt_ready, n)
                    slot_free(act, gv_ready, n, 2)
                    act.activation(xt[:, u, :], ps_t[u][:, :], ACT.Copy).then_inc(xt_copied, 1)
                pipeline(act, TILES // 2, 2, [(0, copy_xt)])
                act.wait_ge(clamped, 1)
                act.activation(rn[:, :, :], inv[:, :, :], ACT.Sqrt).then_inc(rooted, 1)
                act.wait_ge(clamped, 2)
                act.activation(ln[:, :, :], n2[:, :, :], ACT.Ln).then_inc(logged, 1)

            @block.vector
            def _(dve):
                dve.memset(va[:, :, :, HD:HD + 1], 1.0).then_inc(ones_set, 1)
                dve.wait_ge(b_loaded, 16)

                def add_bias(k, u):
                    n = 2 * k + u
                    item_done(dve, gv_ready, n)
                    dve.tensor_tensor(gv[:, n, :], ps_gv[u][:, 0:D], bias[:, 0:D], ALU.add).then_inc(g_biased, 1)
                    dve.tensor_tensor(va[:, n, :, 0:HD],
                                      ps_gv[u][:, D:2 * D].rearrange("p (h d) -> p h d", h=H),
                                      bias[:, D:2 * D].rearrange("p (h d) -> p h d", h=H),
                                      ALU.add).then_inc(v_biased, 1)

                def sum_squares(k, u):
                    n = 2 * k + u
                    item_done(dve, squared, n)
                    dve.tensor_reduce(n2[:, n, :], sq[:, u, :].rearrange("p (h d) -> p h d", h=H),
                                      AX.X, ALU.add).then_inc(summed, 1)
                pipeline(dve, TILES // 2, 2, [(0, add_bias), (1, sum_squares)])
                dve.wait_ge(summed, TILES)
                dve.tensor_scalar(lo[:, :, :], n2[:, :, :], 2.0 ** -115, None, ALU.max).then_inc(floored, 1)
                dve.wait_ge(floored, 1)
                dve.reciprocal(inv[:, :, :], lo[:, :, :]).then_inc(clamped, 1)
                dve.tensor_scalar(n2[:, :, :], n2[:, :, :], 2.0 ** -63, 2.0 ** 63, ALU.max, ALU.min).then_inc(clamped, 1)

            @block.gpsimd
            def _(pool):
                identity_f32(nc, pool, ident, made)

                def square(k, u):
                    n = 2 * k + u
                    item_done(pool, g_biased, n)
                    slot_free(pool, summed, n, 2)
                    pool.tensor_tensor(sq[:, u, :], gv[:, n, :], gv[:, n, :], ALU.mult).then_inc(squared, 1)
                pipeline(pool, TILES // 2, 2, [(0, square)])
        kit.clear_semaphores()


def l0_attn_heads(nc, gv, va, rn, ln, ident, att_out):
    with ExitStack() as stack:
        kit = Kit(nc, stack, "l0ah")
        pad = kit.sb("pad", [P, 2, 2, 4, 32])
        pad2 = kit.sb("pad2", [P, 2, 2, 4, 32])
        only_g = kit.sb("only_g", [P, 1])
        ones = kit.sb("ones", [P, P])
        lhs = kit.sb("lhs", [P, 2, 2, P])
        rhs = kit.sb("rhs", [P, 2, 2, 2, P])
        masks = kit.sb("masks", [P, 2, P])
        lower, upper = masks[:, 0, :], masks[:, 1, :]
        g_zeroed, g_set = kit.sem("g_zeroed"), kit.sem("g_set")
        masks_cut = kit.sem("masks_cut")

        def heads(mask):
            return mask.unsqueeze(1).to_broadcast([P, HALF, P])

        f = kit.sb("f", [P, 2, HALF, P])
        c = kit.sb("c", [P, 2, HALF, P])
        cm = kit.sb("cm", [P, 2, HALF, P])
        wt = kit.sb("wt", [P, 2, HALF, P])
        e = kit.sb("e", [P, 2, HALF, P])
        em = kit.sb("em", [P, 2, HALF, P])
        st = kit.sb("st", [P, 2, 6, HALF])
        o = kit.sb("o", [P, 2, HALF, HD])
        ps_a = kit.ps("ps_a", [P, 4, P])
        ps_s = kit.ps("ps_s", [P, 4, 2, 2, P])
        ps_f = kit.ps("ps_f", [P, HALF, P])
        ps_o = kit.ps("ps_o", [P, 512])
        names = ("preset", "zeroed", "padded", "lnput", "transposed", "lhs_copied", "rhs_copied", "scored", "tanh_done",
                 "corr_done", "corr_masked", "rows_summed", "denom_done", "inv_done", "inv_summed", "suminv_done",
                 "fit_done", "fit_spread", "weighted", "exped", "exp_masked", "applied", "rowsum_inv", "normalised")
        (preset, zeroed, padded, lnput, transposed, lhs_copied, rhs_copied, scored, tanh_done,
         corr_done, corr_masked, rows_summed, denom_done, inv_done, inv_summed, suminv_done,
         fit_done, fit_spread, weighted, exped, exp_masked, applied, rowsum_inv, normalised) = (kit.sem(n) for n in names)
        o_stored = [kit.sem(f"o_stored{u}") for u in range(2)]

        with nc.Block() as block:
            @block.gpsimd
            def _(pool):
                pool.memset(pad[:, :, :, :, :], 0.0).then_inc(zeroed, 1)
                pool.memset(pad2[:, :, :, :, :], 0.0).then_inc(zeroed, 1)
                pool.memset(ones[:, :], 1.0).then_inc(preset, 1)
                pool.memset(masks[:, :, :], 1.0).then_inc(zeroed, 1)
                pool.wait_ge(zeroed, 3)
                pool.affine_select(out=lower, in_=lower, compare_op=ALU.is_ge, fill=0.0, base=0,
                                   pattern=[[-1, P]], channel_multiplier=1).then_inc(masks_cut, 1)
                pool.affine_select(out=upper, in_=upper, compare_op=ALU.is_ge, fill=0.0, base=0,
                                   pattern=[[1, P]], channel_multiplier=-1).then_inc(masks_cut, 1)
                pool.wait_ge(masks_cut, 2)
                pool.memset(pad[:, :, :, :, HD + 1:HD + 2], 1.0).then_inc(preset, 1)
                pool.memset(pad2[:, :, :, :, HD:HD + 1], 1.0).then_inc(preset, 1)

                def mask_corr(k, u):
                    n = 2 * k + u
                    item_done(pool, corr_done, n)
                    slot_free(pool, rows_summed, n, 2)
                    pool.tensor_tensor(cm[:, u, :, :], c[:, u, :, :], heads(lower), ALU.mult).then_inc(corr_masked, 1)

                def mask_exp(k, u):
                    n = 2 * k + u
                    item_done(pool, exped, n)
                    slot_free(pool, applied, n, 2)
                    pool.tensor_tensor(em[:, u, :, :], e[:, u, :, :], heads(upper), ALU.mult).then_inc(exp_masked, 1)
                pipeline(pool, TILES, 2, [(1, mask_corr), (3, mask_exp)])

            @block.vector
            def _(dve):
                dve.memset(only_g[:, :], 0.0).then_inc(g_zeroed, 1)
                dve.wait_ge(g_zeroed, 1)
                for r in range(4):
                    ins = dve.memset(only_g[32 * r:32 * r + HD, :], 1.0)
                ins.then_inc(g_set, 1)
                dve.wait_ge(preset, 3)

                def unit_vectors(k, u):
                    n = 2 * k + u
                    slot_free(dve, transposed, n, 2)
                    g = gv[:, k, u * P:(u + 1) * P].rearrange("p (g r d) -> p g r d", g=2, r=4)
                    r = rn[:, k, HALF * u:HALF * u + HALF].rearrange("p (g r) -> p g r", g=2)
                    for gg in range(2):
                        ins = dve.tensor_tensor(pad[:, u, gg, :, 0:HD], g[:, gg, :, :], spread(r[:, gg, :], HD), ALU.mult)
                    ins.then_inc(padded, 1)
                    l = ln[:, k, HALF * u:HALF * u + HALF].rearrange("p (g r) -> p g r", g=2).unsqueeze(3)
                    dve.tensor_scalar(pad[:, u, :, :, HD:HD + 1], l, 0.5, -math.log(1e-8), ALU.mult, ALU.add)
                    dve.tensor_scalar(pad2[:, u, :, :, HD + 1:HD + 2], l, 0.5, None, ALU.mult).then_inc(lnput, 1)

                def correlate(k, u):
                    n = 2 * k + u
                    item_done(dve, tanh_done, n)
                    slot_free(dve, corr_masked, n, 2)
                    slot_free(dve, weighted, n, 2)
                    for r in range(4):
                        ins = dve.scalar_tensor_tensor(out=c[:, u, 2 * r:2 * r + 2, :], in0=f[:, u, 2 * r:2 * r + 2, :],
                                                       scalar=1.0, in1=ps_s[:, r, :, 0, :], op0=ALU.add, op1=ALU.mult)
                    ins.then_inc(corr_done, 1)

                def row_sums(k, u):
                    n = 2 * k + u
                    item_done(dve, corr_masked, n)
                    dve.tensor_reduce(st[:, u, 0, :], cm[:, u, :, :], AX.X, ALU.add).then_inc(rows_summed, 1)
                    item_done(dve, rows_summed, n)
                    dve.tensor_scalar(st[:, u, 1, :], st[:, u, 0, :], 0.25 / S, 1.0, ALU.mult, ALU.add).then_inc(denom_done, 1)
                    item_done(dve, denom_done, n)
                    slot_free(dve, inv_summed, n, 2)
                    dve.reciprocal(st[:, u, 2, :], st[:, u, 1, :]).then_inc(inv_done, 1)

                def fitness(k, u):
                    n = 2 * k + u
                    item_done(dve, inv_summed, n)
                    dve.reciprocal(st[:, u, 3, :], ps_f[:, 0, 0:HALF]).then_inc(suminv_done, 1)
                    item_done(dve, suminv_done, n)
                    slot_free(dve, fit_spread, n, 2)
                    dve.tensor_tensor(st[:, u, 4, :], st[:, u, 2, :], st[:, u, 3, :], ALU.mult).then_inc(fit_done, 1)

                def weigh(k, u):
                    n = 2 * k + u
                    item_done(dve, fit_spread, n)
                    slot_free(dve, exped, n, 2)
                    dve.tensor_tensor(wt[:, u, :, :], ps_f[:, :, :], c[:, u, :, :], ALU.mult).then_inc(weighted, 1)

                def normalise(k, u):
                    n = 2 * k + u
                    item_done(dve, applied, n)
                    po = ps_o[:, 0:HALF * (HD + 1)].rearrange("p (h d) -> p h d", d=HD + 1)
                    dve.reciprocal(st[:, u, 5, :], po[:, :, HD]).then_inc(rowsum_inv, 1)
                    item_done(dve, rowsum_inv, n)
                    slot_free(dve, o_stored[u], k, 1, 16)
                    dve.tensor_tensor(o[:, u, :, :], po[:, :, 0:HD], spread(st[:, u, 5, :], HD), ALU.mult).then_inc(normalised, 1)
                pipeline(dve, TILES, 2, [(0, unit_vectors), (3, weigh), (1, correlate), (2, row_sums), (2, fitness),
                                         (4, normalise)])

            @block.tensor
            def _(pe):
                def transposes(k, u):
                    n = 2 * k + u
                    item_done(pe, padded, n)
                    item_done(pe, lnput, n)
                    slot_free(pe, rhs_copied, n, 1)
                    for g in range(2):
                        pe.transpose(ps_a[:, g, :], pad[:, u, g, :, :].rearrange("p r d -> p (r d)"), ident[:, :])
                        last = pe.transpose(ps_a[:, 2 + g, :], pad2[:, u, g, :, :].rearrange("p r d -> p (r d)"), ident[:, :])
                    last.then_inc(transposed, 1)

                def score(k, u):
                    n = 2 * k + u
                    item_done(pe, rhs_copied, n)
                    slot_free(pe, corr_done, n, 1)
                    for g in range(2):
                        for r in range(4):
                            last = pe.matmul(ps_s[:, r, g, :, :], lhs[32 * r:32 * r + 32, u, g, :],
                                             rhs[32 * r:32 * r + 32, u, g, :, :], start=True, stop=True)
                    last.then_inc(scored, 1)

                def sum_inverse(k, u):
                    n = 2 * k + u
                    item_done(pe, inv_done, n)
                    slot_free(pe, weighted, n, 1)
                    pe.matmul(ps_f[:, 0, 0:HALF], ones[:, :], st[:, u, 2, :], start=True, stop=True).then_inc(inv_summed, 1)

                def spread_fitness(k, u):
                    n = 2 * k + u
                    item_done(pe, fit_done, n)
                    for h in range(HALF):
                        last = pe.transpose(ps_f[:, h, :], st[:, u, 4, h:h + 1].to_broadcast([P, P]), ident[:, :])
                    last.then_inc(fit_spread, 1)

                def apply(k, u):
                    n = 2 * k + u
                    item_done(pe, exp_masked, n)
                    slot_free(pe, normalised, n, 1)
                    for h in range(HALF):
                        head = HALF * u + 4 * (h % 2) + h // 2
                        at = (4 * (h % 2) + h // 2) * (HD + 1)
                        last = pe.matmul(ps_o[:, at:at + HD + 1], em[:, u, h, :], va[:, k, head, :],
                                         start=True, stop=True)
                    last.then_inc(applied, 1)
                pipeline(pe, TILES, 2, [(0, transposes), (4, apply), (0, score), (2, sum_inverse), (2, spread_fitness)])

            @block.scalar
            def _(act):
                def copy_operands(k, u):
                    n = 2 * k + u
                    item_done(act, transposed, n)
                    slot_free(act, scored, n, 2)
                    act.activation(lhs[:, u, :, :], ps_a[:, 0:2, :], ACT.Copy).then_inc(lhs_copied, 1)
                    act.activation(rhs[:, u, :, 0, :], ps_a[:, 0:2, :], ACT.Copy, scale=only_g[:, :])
                    act.activation(rhs[:, u, :, 1, :], ps_a[:, 2:4, :], ACT.Copy).then_inc(rhs_copied, 1)

                def guard(k, u):
                    n = 2 * k + u
                    item_done(act, scored, n)
                    slot_free(act, corr_done, n, 2)
                    for r in range(4):
                        ins = act.activation(f[:, u, 2 * r:2 * r + 2, :], ps_s[:, r, :, 1, :], ACT.Tanh, scale=0.5)
                    ins.then_inc(tanh_done, 1)

                def exponentials(k, u):
                    n = 2 * k + u
                    item_done(act, weighted, n)
                    slot_free(act, exp_masked, n, 2)
                    act.activation(e[:, u, :, :], wt[:, u, :, :], ACT.Exp, scale=0.25).then_inc(exped, 1)
                act.wait_ge(g_set, 1)
                pipeline(act, TILES, 2, [(1, guard), (0, copy_operands), (3, exponentials)])

            @block.sync
            def _(sp):
                def store(k, u):
                    item_done(sp, normalised, 2 * k + u)
                    sp.dma_start(att_out[k, :, u * P:(u + 1) * P], o[:, u, :, :].rearrange("p h d -> p (h d)")).then_inc(o_stored[u], 16)
                pipeline(sp, TILES, 2, [(4, store)])
                for u in range(2):
                    sp.wait_ge(o_stored[u], 16 * TILES)
        kit.clear_semaphores()


class NormSteps:

    def __init__(self, kit):
        self.stats = kit.sb("ln_stats", [P, 2, 6])
        self.mv = kit.sb("ln_mv", [P, 2, 2])
        self.ve = kit.sb("ln_ve", [P, 2, 1])
        self.rstd = kit.sb("ln_rstd", [P, 2, 1])
        self.half = kit.sb("ln_half", [P, 1])
        self.spare = kit.sb("ln_spare", [P, 1])
        self.eps = kit.sb("ln_eps", [P, 1])
        self.half_set = kit.sem("ln_half_set")
        self.stats_done, self.mv_done = kit.sem("ln_stats_done"), kit.sem("ln_mv_done")
        self.ve_done, self.rstd_done = kit.sem("ln_ve_done"), kit.sem("ln_rstd_done")

    def preset(self, pool):
        pool.memset(self.half[:, :], -0.5).then_inc(self.half_set, 1)
        pool.memset(self.eps[:, :], LN_EPS).then_inc(self.half_set, 1)
        pool.wait_ge(self.half_set, 2)

    def statistics(self, dve, r, n, u, normed):
        dve.bn_stats(self.stats[:, u, :], r).then_inc(self.stats_done, 1)
        item_done(dve, self.stats_done, n)
        slot_free(dve, normed, n, 2)
        if type(n) is not int:
            dve.memset(self.spare[:, :], 0.0)
        dve.bn_aggr(self.mv[:, u, :], self.stats[:, u, :]).then_inc(self.mv_done, 1)

    def root(self, pool, n, u, normed):
        item_done(pool, self.mv_done, n)
        pool.tensor_tensor(self.ve[:, u, :], self.mv[:, u, 1:2], self.eps[:, :], ALU.add).then_inc(self.ve_done, 1)
        item_done(pool, self.ve_done, n)
        slot_free(pool, normed, n, 2)
        pool.tensor_tensor(self.rstd[:, u, :], self.ve[:, u, :], self.half[:, :], ALU.pow).then_inc(self.rstd_done, 1)

    def apply(self, dve, out, r, n, u, normed):
        item_done(dve, self.rstd_done, n)
        dve.tensor_scalar(out, r, self.mv[:, u, 0:1], self.rstd[:, u, :], ALU.subtract, ALU.mult).then_inc(normed, 1)


def attention_output(nc, name, att, w, bo, x_in, x_out):
    feats = att.shape[2]
    chunks = feats // P
    with ExitStack() as stack:
        kit = Kit(nc, stack, name)
        ident = kit.sb("ident", [P, P])
        wo = kit.sb("wo", [P, chunks, D])
        bias = kit.sb("bias", [P, D])
        a = kit.sb("a", [P, 2, feats])
        at = kit.sb("at", [P, 2, feats])
        x = kit.sb("x", [P, 2, D])
        xb = kit.sb("xb", [P, 2, D])
        r = kit.sb("r", [P, 2, D])
        y = kit.sb("y", [P, 2, D])
        ps_t = [kit.ps(f"ps_t{u}", [P, feats]) for u in range(2)]
        ps_y = [kit.ps(f"ps_y{u}", [P, D]) for u in range(2)]
        w_loaded, b_loaded, made = kit.sem("w_loaded"), kit.sem("b_loaded"), kit.sem("ident_made")
        a_loaded = [kit.sem(f"a_loaded{u}") for u in range(2)]
        x_loaded = [kit.sem(f"x_loaded{u}") for u in range(2)]
        stored = [kit.sem(f"stored{u}") for u in range(2)]
        transposed, at_copied, projected = kit.sem("transposed"), kit.sem("at_copied"), kit.sem("projected")
        x_biased, residual_done, normed = kit.sem("x_biased"), kit.sem("residual_done"), kit.sem("normed")
        norm = NormSteps(kit)

        with nc.Block() as block:
            @block.sync
            def _(sp):
                sp.dma_start(wo[:, :, :], w.rearrange("(k p) n -> p k n", p=P)).then_inc(w_loaded, 16)
                sp.dma_start(bias[:, :], bcast(bo)).then_inc(b_loaded, 16)

                def load(k, u):
                    n = 2 * k + u
                    slot_free(sp, transposed, n, 2)
                    sp.dma_start(a[:, u, :], att[n, :, :]).then_inc(a_loaded[u], 16)
                    slot_free(sp, x_biased, n, 2)
                    sp.dma_start(x[:, u, :], x_in[n, :, :]).then_inc(x_loaded[u], 16)
                pipeline(sp, TILES // 2, 2, [(0, load)])

            @block.tensor
            def _(pe):
                pe.wait_ge(made, 2)

                def transposes(k, u):
                    n = 2 * k + u
                    item_done(pe, a_loaded[u], k, 16)
                    slot_free(pe, at_copied, n, 2)
                    for c in range(chunks):
                        last = pe.transpose(ps_t[u][:, c * P:(c + 1) * P], a[:, u, c * P:(c + 1) * P], ident[:, :])
                    last.then_inc(transposed, 1)

                def project(k, u):
                    n = 2 * k + u
                    if type(n) is int and n == 0:
                        pe.wait_ge(w_loaded, 16)
                    item_done(pe, at_copied, n)
                    slot_free(pe, residual_done, n, 2)
                    for c in range(chunks):
                        last = pe.matmul(ps_y[u][:, :], at[:, u, c * P:(c + 1) * P], wo[:, c, :],
                                         start=c == 0, stop=c == chunks - 1)
                    last.then_inc(projected, 1)
                pipeline(pe, TILES // 2, 2, [(0, transposes), (1, project)])

            @block.scalar
            def _(act):
                def copy_at(k, u):
                    n = 2 * k + u
                    item_done(act, transposed, n)
                    slot_free(act, projected, n, 2)
                    act.activation(at[:, u, :], ps_t[u][:, :], ACT.Copy).then_inc(at_copied, 1)

                def store(k, u):
                    n = 2 * k + u
                    item_done(act, normed, n)
                    act.dma_start(x_out[n, :, :], y[:, u, :]).then_inc(stored[u], 16)
                pipeline(act, TILES // 2, 2, [(0, copy_at), (3, store)])
                for u in range(2):
                    act.wait_ge(stored[u], 16 * TILES // 2)

            @block.gpsimd
            def _(pool):
                identity_f32(nc, pool, ident, made)
                norm.preset(pool)
                pool.wait_ge(b_loaded, 16)

                def bias_x(k, u):
                    n = 2 * k + u
                    item_done(pool, x_loaded[u], k, 16)
                    slot_free(pool, residual_done, n, 2)
                    pool.tensor_tensor(xb[:, u, :], x[:, u, :], bias[:, :], ALU.add).then_inc(x_biased, 1)

                def root(k, u):
                    norm.root(pool, 2 * k + u, u, normed)
                pipeline(pool, TILES // 2, 2, [(1, root), (0, bias_x)])

            @block.vector
            def _(dve):
                def residual(k, u):
                    n = 2 * k + u
                    item_done(dve, projected, n)
                    item_done(dve, x_biased, n)
                    slot_free(dve, normed, n, 2)
                    dve.tensor_tensor(r[:, u, :], ps_y[u][:, :], xb[:, u, :], ALU.add).then_inc(residual_done, 1)
                    item_done(dve, residual_done, n)
                    norm.statistics(dve, r[:, u, :], n, u, normed)

                def apply(k, u):
                    n = 2 * k + u
                    slot_free(dve, stored[u], k, 1, 16)
                    norm.apply(dve, y[:, u, :], r[:, u, :], n, u, normed)
                pipeline(dve, TILES // 2, 2, [(0, residual), (1, apply)])
        kit.clear_semaphores()


def l0_xattn(nc, x_in, ctx, wq, wk, wv, bq, bk, bv, att_out):
    with ExitStack() as stack:
        kit = Kit(nc, stack, "l0x")
        ident = kit.sb("ident", [P, P])
        identb = kit.sb("identb", [P, P], BF16)
        band = kit.sb("band", [P, 4, P])
        bandb = kit.sb("bandb", [P, 4, P], BF16)
        w_qk = kit.sb("w_qk", [P, 2, 2, 4 * P])
        w_v = kit.sb("w_v", [P, 2, D])
        b_qk = kit.sb("b_qk", [P, 2, 4])
        b_v = kit.sb("b_v", [P, D])
        xc = kit.sb("xc", [P, 2, 2, D])
        xct = kit.sb("xct", [P, 2, 2, D])
        qkt = kit.sb("qkt", [P, 2, 2, 4, P])
        va = kit.sb("va", [P, 2, H, HD + 1])
        sx = kit.sb("sx", [P, 2, HALF, P])
        e = kit.sb("e", [P, 2, HALF, P])
        et = kit.sb("et", [P, 2, HALF, P])
        st = kit.sb("st", [P, 2, 2, HALF])
        o = kit.sb("o", [P, 2, HALF, HD])
        ps_t = kit.ps("ps_t", [P, 4, P])
        ps_qk = kit.ps("ps_qk", [P, 4, P])
        ps_s = kit.ps("ps_s", [P, 4, 4, P])
        ps_e = kit.ps("ps_e", [P, 4, P])
        ps_o = kit.ps("ps_o", [P, 512])
        names = ("made", "made_b", "band_set", "band_cut", "band_ready", "weights_loaded", "ones_set", "xct_ready",
                 "xct_copied", "qk_projected", "v_projected", "qk_biased", "v_biased", "scored", "maxed", "shifted",
                 "exped", "low_transposed", "high_transposed", "et_low_copied", "et_high_copied", "applied", "rowsum_inv", "normalised")
        (made, made_b, band_set, band_cut, band_ready, weights_loaded, ones_set, xct_ready,
         xct_copied, qk_projected, v_projected, qk_biased, v_biased, scored, maxed, shifted,
         exped, low_transposed, high_transposed, et_low_copied, et_high_copied, applied, rowsum_inv, normalised) = (kit.sem(n) for n in names)
        xc_loaded = [[kit.sem(f"{c}_loaded{b}") for b in range(2)] for c in ("x", "ctx")]
        o_stored = [kit.sem(f"o_stored{u}") for u in range(2)]

        with nc.Block() as block:
            @block.gpsimd
            def _(pool):
                identity_f32(nc, pool, ident, made)
                pool.memset(band[:, :, :], 0.0).then_inc(band_set, 1)
                pool.wait_ge(band_set, 1)
                pool.affine_select(out=band[:, :, :], in_=band[:, :, :], compare_op=ALU.is_ge, fill=-1e30, base=64,
                                   pattern=[[0, 4], [-1, P]], channel_multiplier=1).then_inc(band_cut, 1)
                pool.wait_ge(band_cut, 1)
                pool.affine_select(out=band[:, :, :], in_=band[:, :, :], compare_op=ALU.is_ge, fill=-1e30, base=64,
                                   pattern=[[0, 4], [1, P]], channel_multiplier=-1).then_inc(band_cut, 1)

            @block.sync
            def _(sp):
                for i, (dst, src) in enumerate((
                        (w_qk[:, :, 0, :], wq.rearrange("(k p) n -> p k n", p=P)),
                        (w_qk[:, :, 1, :], wk.rearrange("(k p) n -> p k n", p=P)),
                        (w_v[:, :, :], wv.rearrange("(k p) n -> p k n", p=P)),
                        (b_qk[:, 0, :], bq),
                        (b_qk[:, 1, :], bk),
                        (b_v[:, :], bcast(bv)))):
                    sp.dma_start(dst, src).then_inc(weights_loaded, 16)

                def load(k, b):
                    for c, src in enumerate((x_in, ctx)):
                        slot_free(sp, xct_ready, k, 2)
                        sp.dma_start(xc[:, b, c, :], src[k, :, :]).then_inc(xc_loaded[c][b], 16)

                def store(n, k, b, u):
                    item_done(sp, normalised, n)
                    sp.dma_start(att_out[k, :, u * P:(u + 1) * P],
                                 o[:, u, :, :].rearrange("p h d -> p (h d)")).then_inc(o_stored[u], 16)
                pipeline(sp, TILES // 2, 4, [(0, per_tile(load)), (4, per_unit(store))])
                for u in range(2):
                    sp.wait_ge(o_stored[u], 16 * TILES)

            @block.tensor
            def _(pe):
                pe.wait_ge(made, 2)
                pe.wait_ge(band_ready, 1)
                pe.wait_ge(made_b, 1)

                def transposes(k, b):
                    for c in range(2):
                        item_done(pe, xc_loaded[c][b], k // 2, 16)
                    slot_free(pe, v_biased, k, 1)
                    for c in range(4):
                        last = pe.transpose(ps_t[:, c, :], xc[:, b, c // 2, (c % 2) * P:(c % 2 + 1) * P], ident[:, :])
                    last.then_inc(xct_ready, 1)

                def project(k, b, a):
                    slot_free(pe, qk_biased, 2 * k + a, 1)
                    for c in range(4):
                        for kk in range(2):
                            last = pe.matmul(ps_qk[:, c, :], w_qk[:, kk, a, c * P:(c + 1) * P],
                                             xct[:, b, a, kk * P:(kk + 1) * P], start=kk == 0, stop=kk == 1)
                    last.then_inc(qk_projected, 1)

                def project_q(k, b):
                    if type(k) is int and k == 0:
                        pe.wait_ge(weights_loaded, 6 * 16)
                    item_done(pe, xct_copied, k)
                    project(k, b, 0)

                def project_kv(k, b):
                    project(k, b, 1)
                    for kk in range(2):
                        last = pe.matmul(ps_t[:, 0:2, :], xct[:, b, 1, kk * P:(kk + 1) * P], w_v[:, kk, :],
                                         start=kk == 0, stop=kk == 1)
                    last.then_inc(v_projected, 1)

                def score(n, k, b, u):
                    item_done(pe, qk_biased, 2 * k + 1)
                    slot_free(pe, shifted, n, 1)
                    for r in range(4):
                        pe.matmul(ps_s[:, r, 0:2, :], identb[:, :], bandb[:, 0:2, :], start=True, stop=False)
                    for g in range(2):
                        for r in range(4):
                            last = pe.matmul(ps_s[:, r, g, :], qkt[32 * r:32 * r + 32, b, 0, 2 * u + g, :],
                                             qkt[32 * r:32 * r + 32, b, 1, 2 * u + g, :], start=False, stop=g == 1)
                    last.then_inc(scored, 1)

                def transpose_low(n, k, b, u):
                    item_done(pe, exped, n)
                    slot_free(pe, et_high_copied, n, 1)
                    for h in range(4):
                        last = pe.transpose(ps_e[:, h, :], e[:, u, h, :], ident[:, :])
                    last.then_inc(low_transposed, 1)

                def transpose_high(n, k, b, u):
                    item_done(pe, et_low_copied, n)
                    for h in range(4):
                        last = pe.transpose(ps_e[:, h, :], e[:, u, 4 + h, :], ident[:, :])
                    last.then_inc(high_transposed, 1)

                def apply(n, k, b, u):
                    item_done(pe, et_low_copied, n)
                    item_done(pe, et_high_copied, n)
                    item_done(pe, v_biased, k)
                    slot_free(pe, normalised, n, 1)
                    for h in range(HALF):
                        head = 4 * (h % 2) + h // 2
                        last = pe.matmul(ps_o[:, head * (HD + 1):(head + 1) * (HD + 1)], et[:, u, h, :],
                                         va[:, b, HALF * u + head, :], start=True, stop=True)
                    last.then_inc(applied, 1)
                pipeline(pe, TILES // 2, 4, [(1, per_unit(score)), (2, per_unit(transpose_low)), (0, per_tile(transposes)), (0, per_tile(project_q)),
                                           (2, per_unit(transpose_high)),
                                        (3, per_unit(apply)), (0, per_tile(project_kv))])

            @block.scalar
            def _(act):
                act.wait_ge(band_cut, 2)
                act.activation(bandb[:, :, :], band[:, :, :], ACT.Copy).then_inc(band_ready, 1)
                act.wait_ge(made, 2)
                act.activation(identb[:, :], ident[:, :], ACT.Copy).then_inc(made_b, 1)

                def copy_xct(k, b):
                    item_done(act, xct_ready, k)
                    slot_free(act, v_projected, k, 2)
                    act.activation(xct[:, b, :, :].rearrange("p a n -> p (a n)"),
                                   ps_t[:, :, :].rearrange("p a n -> p (a n)"), ACT.Copy).then_inc(xct_copied, 1)

                def exponentials(n, k, b, u):
                    item_done(act, shifted, n)
                    slot_free(act, high_transposed, n, 2)
                    act.activation(e[:, u, :, :], sx[:, u, :, :], ACT.Exp, scale=HD ** -0.5).then_inc(exped, 1)

                def copy_et(n, k, b, u):
                    item_done(act, low_transposed, n)
                    slot_free(act, applied, n, 2)
                    act.activation(et[:, u, 0:4, :], ps_e[:, :, :], ACT.Copy).then_inc(et_low_copied, 1)
                pipeline(act, TILES // 2, 4, [(2, per_unit(copy_et)), (0, per_tile(copy_xct)), (1, per_unit(exponentials))])

            @block.vector
            def _(dve):
                dve.memset(va[:, :, :, HD:HD + 1], 1.0).then_inc(ones_set, 1)
                dve.wait_ge(weights_loaded, 6 * 16)

                def add_bias(k, b, a):
                    item_done(dve, qk_projected, 2 * k + a)
                    dve.tensor_tensor(qkt[:, b, a, :, :], ps_qk[:, :, :], spread(b_qk[:, a, :], P),
                                      ALU.add).then_inc(qk_biased, 1)

                def add_q(k, b):
                    slot_free(dve, scored, 2 * k + 1, 4)
                    add_bias(k, b, 0)

                def add_kv(k, b):
                    add_bias(k, b, 1)
                    item_done(dve, v_projected, k)
                    slot_free(dve, applied, 2 * k + 1, 4)
                    dve.tensor_tensor(va[:, b, :, 0:HD], ps_t[:, 0:2, :].rearrange("p a (h d) -> p (a h) d", d=HD),
                                      b_v[:, :].rearrange("p (h d) -> p h d", d=HD), ALU.add).then_inc(v_biased, 1)

                def shift(n, k, b, u):
                    item_done(dve, scored, n)
                    dve.tensor_reduce(st[:, u, 0, :], ps_s[:, :, 0:2, :], AX.X, ALU.max).then_inc(maxed, 1)
                    item_done(dve, maxed, n)
                    slot_free(dve, exped, n, 2)
                    dve.tensor_tensor(sx[:, u, :, :].rearrange("p (r g) j -> p r g j", g=2), ps_s[:, :, 0:2, :],
                                      st[:, u, 0, :].rearrange("p (r g) -> p r g", g=2).unsqueeze(3).to_broadcast([P, 4, 2, P]),
                                      ALU.subtract).then_inc(shifted, 1)

                def copy_et(n, k, b, u):
                    item_done(dve, high_transposed, n)
                    slot_free(dve, applied, n, 2)
                    dve.tensor_scalar(et[:, u, 4:8, :], ps_e[:, :, :], 1.0, None, ALU.mult).then_inc(et_high_copied, 1)

                def normalise(n, k, b, u):
                    item_done(dve, applied, n)
                    po = ps_o[:, 0:HALF * (HD + 1)].rearrange("p (h d) -> p h d", d=HD + 1)
                    dve.reciprocal(st[:, u, 1, :], po[:, :, HD]).then_inc(rowsum_inv, 1)
                    item_done(dve, rowsum_inv, n)
                    slot_free(dve, o_stored[u], k, 1, 16)
                    dve.tensor_tensor(o[:, u, :, :], po[:, :, 0:HD], spread(st[:, u, 1, :], HD), ALU.mult).then_inc(normalised, 1)
                pipeline(dve, TILES // 2, 4, [(1, per_unit(shift)), (0, per_tile(add_q)), (2, per_unit(copy_et)), (0, per_tile(add_kv)),
                                              (3, per_unit(normalise))])
        kit.clear_semaphores()


def l0_ffn(nc, x_in, w_int, w_scale, bias_row, x_out):
    magic = 1.5 * 2.0 ** 23
    with ExitStack() as stack:
        kit = Kit(nc, stack, "ffn")
        ident = kit.sb("ident", [P, P])
        identb = kit.sb("identb", [P, P], BF16)
        w_i = kit.sb("w_i", [P, 2, D], I32)
        w = kit.sb("w", [P, 2, D], BF16)
        ws = kit.sb("ws", [P, 1])
        wsd = kit.sb("wsd", [P, 1])
        bias = kit.sb("bias", [P, D])
        x = kit.sb("x", [P, 2, D])
        xb = kit.sb("xb", [P, 2, D])
        sq = kit.sb("sq", [P, D])
        st = kit.sb("st", [P, 2, 8])
        half = kit.sb("half", [P, 1])
        xs = kit.sb("xs", [P, 2, D])
        xq = kit.sb("xq", [P, 2, D], BF16)
        xqt = kit.sb("xqt", [P, 2, D], BF16)
        r = kit.sb("r", [P, 2, D])
        y = kit.sb("y", [P, 2, D])
        ps_t = [kit.ps(f"ps_t{u}", [P, D], BF16) for u in range(2)]
        ps_y = [kit.ps(f"ps_y{u}", [P, D]) for u in range(2)]
        names = ("made", "made_b", "w_loaded", "w_ready", "wsd_ready", "half_set", "x_biased", "squares_summed", "maxed",
                 "ms_done", "rms_done", "top_done", "top_inv", "scale_done", "yscale_done", "scaled", "quantised",
                 "transposed", "xqt_copied", "multiplied", "residual_done", "normed")
        (made, made_b, w_loaded, w_ready, wsd_ready, half_set, x_biased, squares_summed, maxed,
         ms_done, rms_done, top_done, top_inv, scale_done, yscale_done, scaled, quantised,
         transposed, xqt_copied, multiplied, residual_done, normed) = (kit.sem(n) for n in names)
        x_loaded = [kit.sem(f"x_loaded{u}") for u in range(2)]
        stored = [kit.sem(f"stored{u}") for u in range(2)]
        norm = NormSteps(kit)

        with nc.Block() as block:
            @block.sync
            def _(sp):
                sp.dma_start(w_i[:, :, :], w_int.rearrange("(k p) n -> p k n", p=P)).then_inc(w_loaded, 16)
                sp.dma_start(ws[:, :], bcast(w_scale)).then_inc(w_loaded, 16)
                sp.dma_start(bias[:, :], bcast(bias_row)).then_inc(w_loaded, 16)

                def load(k, u):
                    n = 2 * k + u
                    slot_free(sp, x_biased, n, 2)
                    slot_free(sp, squares_summed, n, 2)
                    slot_free(sp, scaled, n, 2)
                    sp.dma_start(x[:, u, :], x_in[n, :, :]).then_inc(x_loaded[u], 16)
                pipeline(sp, TILES // 2, 2, [(0, load)])

            @block.gpsimd
            def _(pool):
                identity_f32(nc, pool, ident, made)
                norm.preset(pool)
                pool.memset(half[:, :], -0.5).then_inc(half_set, 1)
                pool.wait_ge(half_set, 1)
                pool.wait_ge(w_loaded, 3 * 16)

                def rms(k, u):
                    n = 2 * k + u
                    item_done(pool, ms_done, n)
                    slot_free(pool, scale_done, n, 2)
                    pool.tensor_tensor(st[:, u, 3:4], st[:, u, 2:3], half[:, :], ALU.pow).then_inc(rms_done, 1)

                def bias_x(k, u):
                    n = 2 * k + u
                    item_done(pool, x_loaded[u], k, 16)
                    slot_free(pool, residual_done, n, 2)
                    pool.tensor_tensor(xb[:, u, :], x[:, u, :], bias[:, :], ALU.add).then_inc(x_biased, 1)

                def root(k, u):
                    norm.root(pool, 2 * k + u, u, normed)
                pipeline(pool, TILES // 2, 2, [(0, rms), (0, bias_x), (1, root)])

            @block.scalar
            def _(act):
                act.wait_ge(made, 2)
                act.activation(identb[:, :], ident[:, :], ACT.Copy).then_inc(made_b, 1)
                act.wait_ge(w_loaded, 3 * 16)
                act.activation(w[:, :, :], w_i[:, :, :], ACT.Copy).then_inc(w_ready, 1)

                def sum_squares(k, u):
                    n = 2 * k + u
                    item_done(act, x_loaded[u], k, 16)
                    slot_free(act, squares_summed, n, 1)
                    slot_free(act, ms_done, n, 2)
                    act.activation(sq[:, :], x[:, u, :], ACT.Square, accum_out=st[:, u, 0:1]).then_inc(squares_summed, 1)

                def copy_xqt(k, u):
                    n = 2 * k + u
                    item_done(act, transposed, n)
                    slot_free(act, multiplied, n, 2)
                    act.activation(xqt[:, u, :], ps_t[u][:, :], ACT.Copy).then_inc(xqt_copied, 1)

                def store(k, u):
                    n = 2 * k + u
                    item_done(act, normed, n)
                    act.dma_start(x_out[n, :, :], y[:, u, :]).then_inc(stored[u], 16)
                pipeline(act, TILES // 2, 2, [(0, sum_squares), (1, copy_xqt), (3, store)])
                for u in range(2):
                    act.wait_ge(stored[u], 16 * TILES // 2)

            @block.tensor
            def _(pe):
                pe.wait_ge(made_b, 1)
                pe.wait_ge(w_ready, 1)

                def transposes(k, u):
                    n = 2 * k + u
                    item_done(pe, quantised, n)
                    slot_free(pe, xqt_copied, n, 2)
                    for c in range(2):
                        last = pe.transpose(ps_t[u][:, c * P:(c + 1) * P], xq[:, u, c * P:(c + 1) * P], identb[:, :])
                    last.then_inc(transposed, 1)

                def multiply(k, u):
                    n = 2 * k + u
                    item_done(pe, xqt_copied, n)
                    slot_free(pe, residual_done, n, 2)
                    for c in range(2):
                        last = pe.matmul(ps_y[u][:, :], xqt[:, u, c * P:(c + 1) * P], w[:, c, :], start=c == 0, stop=c == 1)
                    last.then_inc(multiplied, 1)
                pipeline(pe, TILES // 2, 2, [(0, transposes), (1, multiply)])

            @block.vector
            def _(dve):
                dve.wait_ge(w_loaded, 3 * 16)
                dve.tensor_scalar(wsd[:, :], ws[:, :], 1.0 / 127.0, None, ALU.mult).then_inc(wsd_ready, 1)
                dve.wait_ge(wsd_ready, 1)

                def statistics(k, u):
                    n = 2 * k + u
                    item_done(dve, squares_summed, n)
                    dve.tensor_reduce(st[:, u, 1:2], x[:, u, :], AX.X, ALU.max, apply_absolute_value=True).then_inc(maxed, 1)
                    slot_free(dve, rms_done, n, 2)
                    dve.tensor_scalar(st[:, u, 2:3], st[:, u, 0:1], 1.0 / D, 1e-6, ALU.mult, ALU.add).then_inc(ms_done, 1)

                def quantise(k, u):
                    n = 2 * k + u
                    item_done(dve, rms_done, n)
                    item_done(dve, maxed, n)
                    dve.tensor_scalar(st[:, u, 4:5], st[:, u, 1:2], st[:, u, 3:4], 1e-5, ALU.mult, ALU.max).then_inc(top_done, 1)
                    item_done(dve, top_done, n)
                    dve.reciprocal(st[:, u, 5:6], st[:, u, 4:5]).then_inc(top_inv, 1)
                    item_done(dve, top_inv, n)
                    dve.tensor_scalar(st[:, u, 6:7], st[:, u, 5:6], st[:, u, 3:4], 127.0, ALU.mult, ALU.mult).then_inc(scale_done, 1)
                    slot_free(dve, residual_done, n, 2)
                    dve.tensor_tensor(st[:, u, 7:8], st[:, u, 4:5], wsd[:, :], ALU.mult).then_inc(yscale_done, 1)
                    item_done(dve, scale_done, n)
                    slot_free(dve, quantised, n, 2)
                    dve.tensor_scalar(xs[:, u, :], x[:, u, :], st[:, u, 6:7], magic, ALU.mult, ALU.add).then_inc(scaled, 1)
                    item_done(dve, scaled, n)
                    slot_free(dve, transposed, n, 2)
                    dve.tensor_scalar(xq[:, u, :], xs[:, u, :], magic, 127.0, ALU.subtract, ALU.min).then_inc(quantised, 1)

                def residual(k, u):
                    n = 2 * k + u
                    item_done(dve, multiplied, n)
                    item_done(dve, x_biased, n)
                    item_done(dve, yscale_done, n)
                    slot_free(dve, normed, n, 2)
                    dve.scalar_tensor_tensor(out=r[:, u, :], in0=ps_y[u][:, :], scalar=st[:, u, 7:8], in1=xb[:, u, :],
                                             op0=ALU.mult, op1=ALU.add).then_inc(residual_done, 1)
                    item_done(dve, residual_done, n)
                    norm.statistics(dve, r[:, u, :], n, u, normed)

                def apply(k, u):
                    n = 2 * k + u
                    slot_free(dve, stored[u], k, 1, 16)
                    norm.apply(dve, y[:, u, :], r[:, u, :], n, u, normed)
                pipeline(dve, TILES // 2, 2, [(0, statistics), (2, residual), (0, quantise), (3, apply)])
        kit.clear_semaphores()


L, BM, Z, HV, NE = B, S, 128, 512, 16
BQ = P // L


def mega_norm(nc, x_in, ln_w, ln_b, xn_out):
    with ExitStack() as stack:
        kit = Kit(nc, stack, "mn")
        wb = kit.sb("wb", [P, 2, D])
        x = kit.sb("x", [P, 2, D])
        xh = kit.sb("xh", [P, 2, D])
        xw = kit.sb("xw", [P, 2, D])
        y = kit.sb("y", [P, 2, D])
        wb_loaded, normed, scaled, shifted = (kit.sem(n) for n in ("wb_loaded", "normed", "scaled", "shifted"))
        x_loaded = [kit.sem(f"x_loaded{u}") for u in range(2)]
        stored = [kit.sem(f"stored{u}") for u in range(2)]
        norm = NormSteps(kit)

        with nc.Block() as block:
            @block.sync
            def _(sp):
                sp.dma_start(wb[:, 0, :], bcast(ln_w)).then_inc(wb_loaded, 16)
                sp.dma_start(wb[:, 1, :], bcast(ln_b)).then_inc(wb_loaded, 16)

                def load(k, u):
                    n = 2 * k + u
                    slot_free(sp, normed, n, 2)
                    sp.dma_start(x[:, u, :], x_in[n, :, :]).then_inc(x_loaded[u], 16)
                pipeline(sp, TILES // 2, 2, [(0, load)])

            @block.vector
            def _(dve):
                def statistics(k, u):
                    n = 2 * k + u
                    item_done(dve, x_loaded[u], k, 16)
                    norm.statistics(dve, x[:, u, :], n, u, normed)

                def apply(k, u):
                    n = 2 * k + u
                    slot_free(dve, scaled, n, 2)
                    norm.apply(dve, xh[:, u, :], x[:, u, :], n, u, normed)
                pipeline(dve, TILES // 2, 2, [(0, statistics), (1, apply)])

            @block.gpsimd
            def _(pool):
                norm.preset(pool)
                pool.wait_ge(wb_loaded, 32)

                def root(k, u):
                    norm.root(pool, 2 * k + u, u, normed)

                def affine(k, u):
                    n = 2 * k + u
                    item_done(pool, normed, n)
                    slot_free(pool, shifted, n, 2)
                    pool.tensor_tensor(xw[:, u, :], xh[:, u, :], wb[:, 0, :], ALU.mult).then_inc(scaled, 1)
                    item_done(pool, scaled, n)
                    slot_free(pool, stored[u], k, 1, 16)
                    pool.tensor_tensor(y[:, u, :], xw[:, u, :], wb[:, 1, :], ALU.add).then_inc(shifted, 1)
                pipeline(pool, TILES // 2, 2, [(0, root), (1, affine)])

            @block.scalar
            def _(act):
                def store(k, u):
                    n = 2 * k + u
                    item_done(act, shifted, n)
                    act.dma_start(xn_out[n, :, :], y[:, u, :]).then_inc(stored[u], 16)
                pipeline(act, TILES // 2, 2, [(1, store)])
                for u in range(2):
                    act.wait_ge(stored[u], 16 * TILES // 2)
        kit.clear_semaphores()


def mega_conv(nc, xn, ema, gamma, omega, toep, mx_out):
    G, CH = 4, D // 4
    with ExitStack() as stack:
        kit = Kit(nc, stack, "mc")
        prm = kit.sb("prm", [P, 3, 2, NE])
        gm = kit.sb("gm", [P, 2, NE])
        om = kit.sb("om", [P, 2])
        pa = kit.sb("pa", [P, 2, 2, NE])
        q = kit.sb("q", [P, 3, 2, NE])
        cf = kit.sb("cf", [P, 2, 2, NE])
        lag = kit.sb("lag", [P, L])
        arg = kit.sb("arg", [P, 2, NE, L])
        ex = kit.sb("ex", [P, 2, NE, L])
        kr = kit.sb("kr", [P, 2, NE, L])
        kd = kit.sb("kd", [P, 2, L])
        kp = kit.sb("kp", [P, 2, 2 * L - 1])
        t = kit.sb("t", [P, CH, P])
        xg = kit.sb("xg", [P, BM, CH])
        o = kit.sb("o", [P, BM, CH])
        ps = [kit.ps(f"ps{i}", [P, 4, BM]) for i in range(2)]
        names = ("loaded", "x_loaded", "sig_done", "pa_done", "q_done", "log_done", "coef_done", "lag_set", "arg_done",
                 "exp_done", "prod_done", "k_done", "pad_zeroed", "pad_done", "pad_stored", "t_zeroed", "t_loaded",
                 "convolved", "activated", "stored")
        (loaded, x_loaded, sig_done, pa_done, q_done, log_done, coef_done, lag_set, arg_done,
         exp_done, prod_done, k_done, pad_zeroed, pad_done, pad_stored, t_zeroed, t_loaded,
         convolved, activated, stored) = (kit.sem(n) for n in names)

        with nc.Block() as block:
            @block.sync
            def _(sp):
                for i in range(3):
                    sp.dma_start(prm[:, i, :, :], ema[i, :, :].rearrange("(h p) n -> p h n", p=P)).then_inc(loaded, 16)
                sp.dma_start(gm[:, :, :], gamma.rearrange("(h p) n -> p h n", p=P)).then_inc(loaded, 16)
                sp.dma_start(om[:, :], omega).then_inc(loaded, 16)
                for g in range(G):
                    sp.dma_start(xg[L * g:L * g + L, :, :], xn[:, :, CH * g:CH * g + CH]).then_inc(x_loaded, 16)
                sp.wait_ge(pad_done, 2)
                for l in range(L):
                    sp.dma_start(toep[l, :, :].rearrange("(h p) n -> p h n", p=P),
                                 kp[:, :, L - 1 - l:2 * L - 1 - l]).then_inc(pad_stored, 16)
                sp.wait_ge(pad_stored, 16 * L)
                sp.wait_ge(t_zeroed, 1)
                for g in range(G):
                    sp.dma_start(t[L * g:L * g + L, :, L * g:L * g + L],
                                 toep[:, CH * g:CH * g + CH, :]).then_inc(t_loaded, 16)
                sp.wait_ge(activated, CH // 4)
                for g in range(G):
                    sp.dma_start(mx_out[:, :, CH * g:CH * g + CH], o[L * g:L * g + L, :, :]).then_inc(stored, 16)
                sp.wait_ge(stored, 16 * G)

            @block.gpsimd
            def _(pool):
                pool.iota(lag[:, :], pattern=[[1, L]], base=0, channel_multiplier=0,
                          allow_small_or_imprecise_dtypes=True).then_inc(lag_set, 1)
                pool.memset(kp[:, :, 0:L - 1], 0.0).then_inc(pad_zeroed, 1)
                pool.memset(t[:, :, :], 0.0).then_inc(t_zeroed, 1)

            @block.scalar
            def _(act):
                act.wait_ge(loaded, 5 * 16)
                act.activation(pa[:, :, :, :], prm[:, 0:2, :, :], ACT.Sigmoid).then_inc(sig_done, 1)
                act.wait_ge(q_done, 1)
                act.activation(q[:, 2, :, :], q[:, 1, :, :], ACT.Ln).then_inc(log_done, 1)
                act.wait_ge(arg_done, 1)
                act.activation(ex[:, :, :, :], arg[:, :, :, :], ACT.Exp).then_inc(exp_done, 1)
                for i in range(CH // 4):
                    act.wait_ge(convolved, i + 1)
                    act.activation(o[:, :, 4 * i:4 * i + 4].rearrange("p b c -> p c b"), ps[i % 2][:, :, :],
                                   ACT.Silu).then_inc(activated, 1)

            @block.vector
            def _(dve):
                dve.wait_ge(sig_done, 1)
                dve.tensor_tensor(q[:, 0, :, :], pa[:, 0, :, :], pa[:, 1, :, :], ALU.mult).then_inc(pa_done, 1)
                dve.wait_ge(pa_done, 1)
                dve.tensor_scalar(q[:, 1, :, :], q[:, 0, :, :], -1.0, 1.0, ALU.mult, ALU.add).then_inc(q_done, 1)
                dve.tensor_tensor(cf[:, 0, :, :], pa[:, 0, :, :], prm[:, 2, :, :], ALU.mult).then_inc(coef_done, 1)
                dve.wait_ge(coef_done, 1)
                dve.scalar_tensor_tensor(out=cf[:, 1, :, :], in0=cf[:, 0, :, :], scalar=math.sqrt(1.0 / NE),
                                         in1=gm[:, :, :], op0=ALU.mult, op1=ALU.mult).then_inc(coef_done, 1)
                dve.wait_ge(log_done, 1)
                dve.wait_ge(lag_set, 1)
                for h in range(2):
                    ins = dve.tensor_tensor(arg[:, h, :, :], q[:, 2, h, :].unsqueeze(2).to_broadcast([P, NE, L]),
                                            lag[:, :].unsqueeze(1).to_broadcast([P, NE, L]), ALU.mult)
                ins.then_inc(arg_done, 1)
                dve.wait_ge(exp_done, 1)
                dve.wait_ge(coef_done, 2)
                for h in range(2):
                    ins = dve.tensor_tensor(kr[:, h, :, :], ex[:, h, :, :],
                                            cf[:, 1, h, :].unsqueeze(2).to_broadcast([P, NE, L]), ALU.mult)
                ins.then_inc(prod_done, 1)
                dve.wait_ge(prod_done, 1)
                dve.tensor_reduce(kd[:, :, :], kr[:, :, :, :].rearrange("p h n l -> p h l n"), AX.X, ALU.add).then_inc(k_done, 1)
                dve.wait_ge(k_done, 1)
                dve.wait_ge(pad_zeroed, 1)
                dve.tensor_copy(kp[:, :, L:2 * L - 1], kd[:, :, 1:L]).then_inc(pad_done, 1)
                dve.tensor_tensor(kp[:, :, L - 1:L], kd[:, :, 0:1], om[:, :].unsqueeze(2), ALU.add).then_inc(pad_done, 1)

            @block.tensor
            def _(pe):
                pe.wait_ge(x_loaded, 16 * G)
                pe.wait_ge(t_loaded, 16 * G)
                for i in range(CH // 4):
                    if i >= 2:
                        pe.wait_ge(activated, i - 1)
                    for c in range(4):
                        last = pe.matmul(ps[i % 2][:, c, :], t[:, 4 * i + c, :], xg[:, :, 4 * i + c], start=True, stop=True)
                    last.then_inc(convolved, 1)
        kit.clear_semaphores()


def mega_attn(nc, x_in, xn_in, mx_in, m, x_out):
    with ExitStack() as stack:
        kit = Kit(nc, stack, "ma")
        ident = kit.sb("ident", [P, P])
        w_v = kit.sb("w_v", [P, 2, HV])
        w_r = kit.sb("w_r", [P, 2, HV])
        w_uh = kit.sb("w_uh", [P, 2, HV])
        w_z = kit.sb("w_z", [P, 2, Z])
        w_h = kit.sb("w_h", [P, 4, D])
        b_v = kit.sb("b_v", [P, HV])
        b_r = kit.sb("b_r", [P, HV])
        b_uh = kit.sb("b_uh", [P, HV])
        b_h = kit.sb("b_h", [P, D])
        zp = kit.sb("zp", [P, 5])
        zq = kit.sb("zq", [P, 3])
        rot = kit.sb("rot", [P, 2, L])
        ab = kit.sb("ab", [P, 2, 2])
        rr = kit.sb("rr", [P, 2, 2, L])
        rt = kit.sb("rt", [P, 2, P])
        same = kit.sb("same", [P, P])
        bm = kit.sb("bm", [P, P])
        xin = kit.sb("xin", [P, 2, 2, D])
        xt = kit.sb("xt", [P, 2, 4, P])
        x = kit.sb("x", [P, 2, D])
        x2 = kit.sb("x2", [P, 2, D])
        vb, vt, v2 = (kit.sb(n, [P, 2, HV]) for n in ("vb", "vt", "v2"))
        rb, rth, r2 = (kit.sb(n, [P, 2, HV]) for n in ("rb", "rth", "r2"))
        uh = kit.sb("uh", [P, 2, HV])
        ut = kit.sb("ut", [P, 2, D])
        zb, zt, z2, qt, kt = (kit.sb(n, [P, 2, P]) for n in ("zb", "zt", "z2", "qt", "kt"))
        s, e, et = (kit.sb(n, [P, 2, P]) for n in ("s", "e", "et"))
        st = kit.sb("st", [P, 2, 4])
        hr, hrt = kit.sb("hr", [P, 2, HV]), kit.sb("hrt", [P, 2, HV])
        hb, hth, h2, gx, wg, r, y = (kit.sb(n, [P, 2, D]) for n in ("hb", "hth", "h2", "gx", "wg", "r", "y"))
        ps_t = kit.ps("ps_t", [P, 4, P])
        ps_v, ps_r, ps_uh = (kit.ps(n, [P, HV]) for n in ("ps_v", "ps_r", "ps_uh"))
        ps_zs = kit.ps("ps_zs", [P, 2, P])
        ps_e = kit.ps("ps_e", [P, P])
        ps_h = kit.ps("ps_h", [P, HV])
        ps_hy = kit.ps("ps_hy", [P, HV])
        names = ("made", "w_loaded", "zq_done", "rot_done", "rotated", "spread_done", "bias_mm", "bm_done",
                 "xt_ready", "xt_copied", "projected", "z_biased", "v_biased", "r_biased", "uh_biased", "hb_added",
                 "z_tanh", "v_tanh", "r_tanh", "u_tanh", "z_done", "q_done", "k_done", "v_done", "r_done", "scored",
                 "s_biased", "maxed", "exped", "sum_inv", "sum_quart", "e_transposed", "et_copied", "attended",
                 "gated", "hr_transposed", "hrt_copied", "y_ready", "h_biased", "h_tanh", "h_done", "x_doubled",
                 "diff_done", "mixed", "residual_done", "normed")
        (made, w_loaded, zq_done, rot_done, rotated, spread_done, bias_mm, bm_done,
         xt_ready, xt_copied, projected, z_biased, v_biased, r_biased, uh_biased, hb_added,
         z_tanh, v_tanh, r_tanh, u_tanh, z_done, q_done, k_done, v_done, r_done, scored,
         s_biased, maxed, exped, sum_inv, sum_quart, e_transposed, et_copied, attended,
         gated, hr_transposed, hrt_copied, y_ready, h_biased, h_tanh, h_done, x_doubled,
         diff_done, mixed, residual_done, normed) = (kit.sem(n) for n in names)
        xin_loaded = [[kit.sem(f"{c}_loaded{u}") for u in range(2)] for c in ("xn", "mx")]
        x_loaded = [kit.sem(f"x_loaded{u}") for u in range(2)]
        stored = [kit.sem(f"stored{u}") for u in range(2)]
        norm = NormSteps(kit)

        def tiles(a):
            return a.rearrange("l (t b) d -> t l b d", b=BQ)

        loads = [(w_v, m["wv"], 1), (w_r, m["wr"], 1), (w_uh, m["wuh"], 1), (w_z, m["wz"], 1), (w_h, m["wh"], 1)]
        rows = [(b_v, m["bv"]), (b_r, m["br"]), (b_uh, m["buh"]), (b_h, m["bh"])]

        with nc.Block() as block:
            @block.sync
            def _(sp):
                for dst, src, _ in loads:
                    sp.dma_start(dst[:, :, :], src.rearrange("(k p) n -> p k n", p=P)).then_inc(w_loaded, 16)
                for dst, src in rows:
                    sp.dma_start(dst[:, :], bcast(src)).then_inc(w_loaded, 16)
                sp.dma_start(zp[:, :], m["zp"]).then_inc(w_loaded, 16)
                sp.dma_start(rot[:, :, :], m["rot"]).then_inc(w_loaded, 16)
                sp.dma_start(ab[:, :, :], m["ab"]).then_inc(w_loaded, 16)
                sp.dma_start(same[:, :], m["same"]).then_inc(w_loaded, 16)

                def load(k, u):
                    n = 2 * k + u
                    for c, src in enumerate((xn_in, mx_in)):
                        slot_free(sp, xt_ready, n, 2)
                        sp.dma_start(xin[:, u, c, :], tiles(src)[n, :, :, :]).then_inc(xin_loaded[c][u], 16)

                def load_x(k, u):
                    n = 2 * k + u
                    slot_free(sp, diff_done, n, 2)
                    slot_free(sp, x_doubled, n, 2)
                    sp.dma_start(x[:, u, :], tiles(x_in)[n, :, :, :]).then_inc(x_loaded[u], 16)

                def store(k, u):
                    n = 2 * k + u
                    item_done(sp, normed, n)
                    sp.dma_start(tiles(x_out)[n, :, :, :], y[:, u, :]).then_inc(stored[u], 16)
                pipeline(sp, TILES // 2, 2, [(0, load), (1, load_x), (4, store)])
                for u in range(2):
                    sp.wait_ge(stored[u], 16 * TILES // 2)

            @block.gpsimd
            def _(pool):
                identity_f32(nc, pool, ident, made)
                norm.preset(pool)
                pool.wait_ge(w_loaded, 13 * 16)

                def add_hb(k, u):
                    n = 2 * k + u
                    item_done(pool, uh_biased, n)
                    pool.tensor_tensor(uh[:, u, D:2 * D], uh[:, u, D:2 * D], b_h[:, :], ALU.add).then_inc(hb_added, 1)

                def double_x(k, u):
                    n = 2 * k + u
                    item_done(pool, x_loaded[u], k, 16)
                    slot_free(pool, residual_done, n, 2)
                    pool.tensor_tensor(x2[:, u, :], x[:, u, :], x[:, u, :], ALU.add).then_inc(x_doubled, 1)

                def root(k, u):
                    norm.root(pool, 2 * k + u, u, normed)
                pipeline(pool, TILES // 2, 2, [(1, add_hb), (2, double_x), (2, root)])

            @block.scalar
            def _(act):
                def copy_xt(k, u):
                    n = 2 * k + u
                    item_done(act, xt_ready, n)
                    slot_free(act, projected, n, 2)
                    act.activation(xt[:, u, :, :], ps_t[:, :, :], ACT.Copy).then_inc(xt_copied, 1)

                def tanhs(k, u):
                    n = 2 * k + u
                    item_done(act, z_biased, n)
                    slot_free(act, z_done, n, 2)
                    act.activation(zt[:, u, :], zb[:, u, :], ACT.Tanh, scale=0.5).then_inc(z_tanh, 1)
                    item_done(act, v_biased, n)
                    slot_free(act, v_done, n, 2)
                    act.activation(vt[:, u, :], vb[:, u, :], ACT.Tanh, scale=0.5).then_inc(v_tanh, 1)
                    item_done(act, r_biased, n)
                    slot_free(act, r_done, n, 2)
                    act.activation(rth[:, u, :], rb[:, u, :], ACT.Tanh, scale=0.5).then_inc(r_tanh, 1)
                    item_done(act, uh_biased, n)
                    slot_free(act, mixed, n, 2)
                    act.activation(ut[:, u, :], uh[:, u, 0:D], ACT.Tanh, scale=0.5).then_inc(u_tanh, 1)

                def copy_hr(k, u):
                    n = 2 * k + u
                    item_done(act, hr_transposed, n)
                    slot_free(act, y_ready, n, 2)
                    act.activation(hrt[:, u, :], ps_hy[:, :], ACT.Copy).then_inc(hrt_copied, 1)

                def exponentials(k, u):
                    n = 2 * k + u
                    item_done(act, maxed, n)
                    slot_free(act, e_transposed, n, 2)
                    slot_free(act, sum_inv, n, 2)
                    act.activation(e[:, u, :], s[:, u, :], ACT.Exp, bias=st[:, u, 0:1],
                                   accum_out=st[:, u, 1:2]).then_inc(exped, 1)

                def copy_et(k, u):
                    n = 2 * k + u
                    item_done(act, e_transposed, n)
                    slot_free(act, attended, n, 2)
                    act.activation(et[:, u, :], ps_e[:, :], ACT.Copy).then_inc(et_copied, 1)

                def tanh_h(k, u):
                    n = 2 * k + u
                    item_done(act, h_biased, n)
                    slot_free(act, h_done, n, 2)
                    act.activation(hth[:, u, :], hb[:, u, :], ACT.Tanh, scale=0.5).then_inc(h_tanh, 1)
                pipeline(act, TILES // 2, 2, [(0, copy_xt), (1, tanhs), (2, copy_hr), (1, exponentials), (1, copy_et),
                                              (2, tanh_h)])

            @block.vector
            def _(dve):
                dve.wait_ge(w_loaded, 13 * 16)
                dve.tensor_scalar(zq[:, 0:1], zp[:, 1:2], 0.5 * Z ** -0.5, None, ALU.mult)
                dve.tensor_scalar(zq[:, 1:2], zp[:, 2:3], 0.5, None, ALU.mult)
                dve.tensor_scalar(zq[:, 2:3], zp[:, 3:4], Z ** -0.5, None, ALU.mult).then_inc(zq_done, 1)
                for i in range(2):
                    ins = dve.tensor_scalar(rr[:, i, 0, :], rot[:, 0, :], ab[:, i, 0:1], None, ALU.mult)
                ins.then_inc(rot_done, 1)
                dve.wait_ge(rot_done, 1)
                for i in range(2):
                    ins = dve.scalar_tensor_tensor(out=rr[:, i, 1, :], in0=rot[:, 1, :], scalar=ab[:, i, 1:2],
                                                   in1=rr[:, i, 0, :], op0=ALU.mult, op1=ALU.add)
                ins.then_inc(rotated, 1)
                dve.wait_ge(rotated, 1)
                for i in range(2):
                    ins = dve.tensor_copy(rt[:, i, :].rearrange("p (l b) -> p l b", b=BQ),
                                          rr[:, i, 1, :].unsqueeze(2).to_broadcast([P, L, BQ]))
                ins.then_inc(spread_done, 1)
                dve.wait_ge(bias_mm, 1)
                dve.tensor_tensor(bm[:, :], ps_e[:, :], same[:, :], ALU.add).then_inc(bm_done, 1)
                dve.wait_ge(bm_done, 1)
                dve.wait_ge(zq_done, 1)

                def biases(k, u):
                    n = 2 * k + u
                    item_done(dve, projected, n)
                    slot_free(dve, z_done, n, 2)
                    dve.tensor_scalar(zb[:, u, :], ps_zs[:, 0, :], zp[:, 0:1], None, ALU.add).then_inc(z_biased, 1)
                    slot_free(dve, v_done, n, 2)
                    dve.tensor_tensor(vb[:, u, :], ps_v[:, :], b_v[:, :], ALU.add).then_inc(v_biased, 1)
                    slot_free(dve, r_done, n, 2)
                    dve.tensor_tensor(rb[:, u, :], ps_r[:, :], b_r[:, :], ALU.add).then_inc(r_biased, 1)
                    slot_free(dve, h_biased, n, 2)
                    slot_free(dve, u_tanh, n, 2)
                    dve.tensor_tensor(uh[:, u, :], ps_uh[:, :], b_uh[:, :], ALU.add).then_inc(uh_biased, 1)

                def gate(k, u):
                    n = 2 * k + u
                    item_done(dve, attended, n)
                    slot_free(dve, hr_transposed, n, 2)
                    item_done(dve, sum_quart, n)
                    dve.scalar_tensor_tensor(out=hr[:, u, :], in0=ps_h[:, :], scalar=st[:, u, 3:4], in1=r2[:, u, :],
                                             op0=ALU.mult, op1=ALU.mult).then_inc(gated, 1)

                def activate(k, u):
                    n = 2 * k + u
                    item_done(dve, z_tanh, n)
                    dve.scalar_tensor_tensor(out=z2[:, u, :], in0=zt[:, u, :], scalar=1.0, in1=zb[:, u, :],
                                             op0=ALU.add, op1=ALU.mult).then_inc(z_done, 1)
                    item_done(dve, z_done, n)
                    slot_free(dve, scored, n, 2)
                    dve.tensor_scalar(qt[:, u, :], z2[:, u, :], zq[:, 0:1], zq[:, 2:3], ALU.mult, ALU.add).then_inc(q_done, 1)
                    dve.tensor_scalar(kt[:, u, :], z2[:, u, :], zq[:, 1:2], zp[:, 4:5], ALU.mult, ALU.add).then_inc(k_done, 1)
                    item_done(dve, v_tanh, n)
                    slot_free(dve, attended, n, 2)
                    dve.scalar_tensor_tensor(out=v2[:, u, :], in0=vt[:, u, :], scalar=1.0, in1=vb[:, u, :],
                                             op0=ALU.add, op1=ALU.mult).then_inc(v_done, 1)
                    item_done(dve, r_tanh, n)
                    slot_free(dve, gated, n, 2)
                    dve.scalar_tensor_tensor(out=r2[:, u, :], in0=rth[:, u, :], scalar=1.0, in1=rb[:, u, :],
                                             op0=ALU.add, op1=ALU.mult).then_inc(r_done, 1)

                def softmax_max(k, u):
                    n = 2 * k + u
                    item_done(dve, scored, n)
                    slot_free(dve, exped, n, 2)
                    dve.tensor_tensor(s[:, u, :], ps_zs[:, 1, :], bm[:, :], ALU.add).then_inc(s_biased, 1)
                    item_done(dve, s_biased, n)
                    dve.tensor_reduce(st[:, u, 0:1], s[:, u, :], AX.X, ALU.max, negate=True).then_inc(maxed, 1)

                def invert(k, u):
                    n = 2 * k + u
                    item_done(dve, exped, n)
                    dve.reciprocal(st[:, u, 2:3], st[:, u, 1:2]).then_inc(sum_inv, 1)
                    item_done(dve, sum_inv, n)
                    slot_free(dve, gated, n, 2)
                    dve.tensor_scalar(st[:, u, 3:4], st[:, u, 2:3], 0.25, None, ALU.mult).then_inc(sum_quart, 1)

                def bias_h(k, u):
                    n = 2 * k + u
                    item_done(dve, y_ready, n)
                    item_done(dve, hb_added, n)
                    slot_free(dve, h_done, n, 2)
                    dve.tensor_tensor(hb[:, u, :], ps_hy[:, 0:D], uh[:, u, D:2 * D], ALU.add).then_inc(h_biased, 1)

                def mix(k, u):
                    n = 2 * k + u
                    item_done(dve, h_tanh, n)
                    slot_free(dve, diff_done, n, 1)
                    dve.scalar_tensor_tensor(out=h2[:, u, :], in0=hth[:, u, :], scalar=1.0, in1=hb[:, u, :],
                                             op0=ALU.add, op1=ALU.mult).then_inc(h_done, 1)
                    item_done(dve, h_done, n)
                    item_done(dve, x_loaded[u], k, 16)
                    slot_free(dve, mixed, n, 2)
                    dve.scalar_tensor_tensor(out=gx[:, u, :], in0=h2[:, u, :], scalar=0.5, in1=x[:, u, :],
                                             op0=ALU.mult, op1=ALU.subtract).then_inc(diff_done, 1)
                    item_done(dve, diff_done, n)
                    item_done(dve, u_tanh, n)
                    slot_free(dve, residual_done, n, 2)
                    dve.scalar_tensor_tensor(out=wg[:, u, :], in0=ut[:, u, :], scalar=1.0, in1=gx[:, u, :],
                                             op0=ALU.add, op1=ALU.mult).then_inc(mixed, 1)
                    item_done(dve, mixed, n)
                    item_done(dve, x_doubled, n)
                    slot_free(dve, normed, n, 2)
                    dve.scalar_tensor_tensor(out=r[:, u, :], in0=wg[:, u, :], scalar=0.5, in1=x2[:, u, :],
                                             op0=ALU.mult, op1=ALU.add).then_inc(residual_done, 1)
                    item_done(dve, residual_done, n)
                    norm.statistics(dve, r[:, u, :], n, u, normed)

                def apply(k, u):
                    n = 2 * k + u
                    slot_free(dve, stored[u], k, 1, 16)
                    norm.apply(dve, y[:, u, :], r[:, u, :], n, u, normed)
                pipeline(dve, TILES // 2, 2, [(1, biases), (2, gate), (1, activate), (3, apply), (1, softmax_max),
                                              (2, bias_h), (1, invert), (2, mix)])

            @block.tensor
            def _(pe):
                pe.wait_ge(made, 2)
                pe.wait_ge(spread_done, 1)
                pe.matmul(ps_e[:, :], rt[:, 0, :], rt[:, 1, :], start=True, stop=True).then_inc(bias_mm, 1)
                pe.wait_ge(bm_done, 1)
                pe.wait_ge(w_loaded, 13 * 16)

                def transposes(k, u):
                    n = 2 * k + u
                    for c in range(2):
                        item_done(pe, xin_loaded[c][u], k, 16)
                    slot_free(pe, xt_copied, n, 1)
                    for c in range(4):
                        last = pe.transpose(ps_t[:, c, :], xin[:, u, c // 2, (c % 2) * P:(c % 2 + 1) * P], ident[:, :])
                    last.then_inc(xt_ready, 1)

                def attend(k, u):
                    n = 2 * k + u
                    item_done(pe, et_copied, n)
                    item_done(pe, v_done, n)
                    slot_free(pe, gated, n, 1)
                    pe.matmul(ps_h[:, :], et[:, u, :], v2[:, u, :], start=True, stop=True).then_inc(attended, 1)

                def score(k, u):
                    n = 2 * k + u
                    item_done(pe, q_done, n)
                    item_done(pe, k_done, n)
                    pe.matmul(ps_zs[:, 1, :], qt[:, u, :], kt[:, u, :], start=True, stop=True).then_inc(scored, 1)

                def transpose_hr(k, u):
                    n = 2 * k + u
                    item_done(pe, gated, n)
                    slot_free(pe, h_biased, n, 1)
                    for c in range(4):
                        last = pe.transpose(ps_hy[:, c * P:(c + 1) * P], hr[:, u, c * P:(c + 1) * P], ident[:, :])
                    last.then_inc(hr_transposed, 1)

                def transpose_e(k, u):
                    n = 2 * k + u
                    item_done(pe, exped, n)
                    slot_free(pe, et_copied, n, 1)
                    pe.transpose(ps_e[:, :], e[:, u, :], ident[:, :]).then_inc(e_transposed, 1)

                def project_h(k, u):
                    n = 2 * k + u
                    item_done(pe, hrt_copied, n)
                    for c in range(4):
                        last = pe.matmul(ps_hy[:, 0:D], hrt[:, u, c * P:(c + 1) * P], w_h[:, c, :], start=c == 0, stop=c == 3)
                    last.then_inc(y_ready, 1)

                def project(k, u):
                    n = 2 * k + u
                    item_done(pe, xt_copied, n)
                    slot_free(pe, uh_biased, n, 1)
                    slot_free(pe, s_biased, n, 1)
                    for c in range(2):
                        pe.matmul(ps_zs[:, 0, :], w_z[:, c, :], xt[:, u, 2 + c, :], start=c == 0, stop=c == 1)
                    for ps_x, w_x, first in ((ps_v, w_v, 0), (ps_r, w_r, 2), (ps_uh, w_uh, 2)):
                        for c in range(2):
                            last = pe.matmul(ps_x[:, :], xt[:, u, first + c, :], w_x[:, c, :], start=c == 0, stop=c == 1)
                    last.then_inc(projected, 1)
                pipeline(pe, TILES // 2, 2, [(0, transposes), (2, attend), (1, score), (2, transpose_hr), (1, transpose_e),
                                             (2, project_h), (0, project)])
        kit.clear_semaphores()


def l1_xattn(nc, x_in, ctx, w, att_out):
    W, QH = 64, 4
    QF = QH * W
    UNITS = H // QH

    def per_tile8(f):
        return lambda k, u: f(2 * k + u // UNITS, u // UNITS) if u % UNITS == 0 else None

    def per_unit8(f):
        return lambda k, u: f(2 * UNITS * k + u, 2 * k + u // UNITS, u // UNITS, u % UNITS, u % 2)

    with ExitStack() as stack:
        kit = Kit(nc, stack, "l1x")
        ident = kit.sb("ident", [P, P])
        w_qk = kit.sb("w_qk", [P, 2, 2, H * W])
        w_v = kit.sb("w_v", [P, 2, H * W])
        b_qk = kit.sb("b_qk", [P, UNITS, 2, 2])
        b_v = kit.sb("b_v", [P, H * W])
        xc = kit.sb("xc", [P, 2, 2, D])
        xct = kit.sb("xct", [P, 2, 2, D])
        qkt = kit.sb("qkt", [P, 2, 2, 2, P])
        va = kit.sb("va", [P, 4, QH, W + 1])
        sx = kit.sb("sx", [P, 2, QH, P])
        e = kit.sb("e", [P, 2, QH, P])
        et = kit.sb("et", [P, 2, QH, P])
        st = kit.sb("st", [P, 2, 2, QH])
        o = kit.sb("o", [P, 2, QH, W])
        ps_t = kit.ps("ps_t", [P, 4, P])
        ps_qk = [kit.ps(f"ps_qk{i}", [P, 2, 2, P]) for i in range(2)]
        ps_v = kit.ps("ps_v", [P, 512])
        ps_s = kit.ps("ps_s", [P, 2, 4, P])
        ps_e = kit.ps("ps_e", [P, QH, P])
        ps_o = kit.ps("ps_o", [P, 512])
        names = ("made", "weights_loaded", "ones_set", "xct_ready", "xct_copied", "qk_projected", "v_projected",
                 "qk_biased", "v_biased", "scored", "maxed", "shifted", "exped", "e_transposed", "et_copied", "applied",
                 "rowsum_inv", "normalised")
        (made, weights_loaded, ones_set, xct_ready, xct_copied, qk_projected, v_projected,
         qk_biased, v_biased, scored, maxed, shifted, exped, e_transposed, et_copied, applied,
         rowsum_inv, normalised) = (kit.sem(n) for n in names)
        xc_loaded = [[kit.sem(f"{c}_loaded{b}") for b in range(2)] for c in ("x", "ctx")]
        o_stored = [kit.sem(f"o_stored{u}") for u in range(2)]
        rounds = TILES // 2

        with nc.Block() as block:
            @block.gpsimd
            def _(pool):
                identity_f32(nc, pool, ident, made)

            @block.sync
            def _(sp):
                for dst, src in ((w_qk[:, :, 0, :], w["wq"].rearrange("(k p) n -> p k n", p=P)),
                                 (w_qk[:, :, 1, :], w["wk"].rearrange("(k p) n -> p k n", p=P)),
                                 (w_v[:, :, :], w["wv"].rearrange("(k p) n -> p k n", p=P)),
                                 (b_qk[:, :, :, :], w["bqk"]), (b_v[:, :], bcast(w["bv"]))):
                    sp.dma_start(dst, src).then_inc(weights_loaded, 16)

                def load(t, b):
                    for c, src in enumerate((x_in, ctx)):
                        slot_free(sp, xct_ready, t, 2)
                        sp.dma_start(xc[:, b, c, :], src[t, :, :]).then_inc(xc_loaded[c][b], 16)

                def store(n, t, b, j, s):
                    item_done(sp, normalised, n)
                    sp.dma_start(att_out[t, :, QF * j:QF * j + QF],
                                 o[:, s, :, :].rearrange("p h d -> p (h d)")).then_inc(o_stored[s], 16)
                pipeline(sp, rounds, 2 * UNITS, [(0, per_tile8(load)), (4, per_unit8(store))])
                for s in range(2):
                    sp.wait_ge(o_stored[s], 16 * TILES * UNITS // 2)

            @block.tensor
            def _(pe):
                pe.wait_ge(made, 2)

                def transposes(t, b):
                    for c in range(2):
                        item_done(pe, xc_loaded[c][b], t // 2, 16)
                    slot_free(pe, xct_copied, t, 1)
                    for c in range(4):
                        last = pe.transpose(ps_t[:, c, :], xc[:, b, c // 2, (c % 2) * P:(c % 2 + 1) * P], ident[:, :])
                    last.then_inc(xct_ready, 1)

                def project(n, t, b, j, s):
                    if type(n) is int and n == 0:
                        pe.wait_ge(weights_loaded, 5 * 16)
                    item_done(pe, xct_copied, t)
                    slot_free(pe, qk_biased, n, 2)
                    for a in range(2):
                        for c in range(2):
                            for kk in range(2):
                                last = pe.matmul(ps_qk[s][:, a, c, :], w_qk[:, kk, a, QF * j + P * c:QF * j + P * c + P],
                                                 xct[:, b, a, kk * P:(kk + 1) * P], start=kk == 0, stop=kk == 1)
                    last.then_inc(qk_projected, 1)
                    slot_free(pe, v_biased, n, 1)
                    for kk in range(2):
                        last = pe.matmul(ps_v[:, 0:QF], xct[:, b, 1, kk * P:(kk + 1) * P],
                                         w_v[:, kk, QF * j:QF * j + QF], start=kk == 0, stop=kk == 1)
                    last.then_inc(v_projected, 1)

                def score(n, t, b, j, s):
                    item_done(pe, qk_biased, n)
                    slot_free(pe, shifted, n, 1)
                    for c in range(2):
                        for r in range(2):
                            last = pe.matmul(ps_s[:, r, c, :], qkt[W * r:W * r + W, s, 0, c, :],
                                             qkt[W * r:W * r + W, s, 1, c, :], start=True, stop=True)
                    last.then_inc(scored, 1)

                def transpose_e(n, t, b, j, s):
                    item_done(pe, exped, n)
                    slot_free(pe, et_copied, n, 1)
                    for h in range(QH):
                        last = pe.transpose(ps_e[:, h, :], e[:, s, h, :], ident[:, :])
                    last.then_inc(e_transposed, 1)

                def apply(n, t, b, j, s):
                    item_done(pe, et_copied, n)
                    item_done(pe, v_biased, n)
                    slot_free(pe, normalised, n, 1)
                    for h in range(QH):
                        head = 2 * (h % 2) + h // 2
                        last = pe.matmul(ps_o[:, head * (W + 1):(head + 1) * (W + 1)], et[:, s, h, :],
                                         va[:, j, head, :], start=True, stop=True)
                    last.then_inc(applied, 1)
                pipeline(pe, rounds, 2 * UNITS, [(3, per_unit8(transpose_e)), (0, per_tile8(transposes)), (2, per_unit8(score)),
                                                 (1, per_unit8(project)), (3, per_unit8(apply))])

            @block.scalar
            def _(act):
                def copy_xct(t, b):
                    item_done(act, xct_ready, t)
                    slot_free(act, v_projected, UNITS * t + UNITS - 1, 2 * UNITS)
                    act.activation(xct[:, b, :, :].rearrange("p a n -> p (a n)"),
                                   ps_t[:, :, :].rearrange("p a n -> p (a n)"), ACT.Copy).then_inc(xct_copied, 1)

                def exponentials(n, t, b, j, s):
                    item_done(act, shifted, n)
                    slot_free(act, e_transposed, n, 2)
                    act.activation(e[:, s, :, :], sx[:, s, :, :], ACT.Exp, scale=W ** -0.5).then_inc(exped, 1)

                def copy_et(n, t, b, j, s):
                    item_done(act, e_transposed, n)
                    slot_free(act, applied, n, 2)
                    act.activation(et[:, s, :, :], ps_e[:, :, :], ACT.Copy).then_inc(et_copied, 1)
                pipeline(act, rounds, 2 * UNITS, [(3, per_unit8(copy_et)), (0, per_tile8(copy_xct)), (2, per_unit8(exponentials))])

            @block.vector
            def _(dve):
                dve.memset(va[:, :, :, W:W + 1], 1.0).then_inc(ones_set, 1)
                dve.wait_ge(weights_loaded, 5 * 16)

                def add_bias(n, t, b, j, s):
                    item_done(dve, qk_projected, n)
                    slot_free(dve, scored, n, 2)
                    dve.tensor_tensor(qkt[:, s, :, :, :], ps_qk[s][:, :, :, :],
                                      b_qk[:, j, :, :].unsqueeze(3).to_broadcast([P, 2, 2, P]), ALU.add).then_inc(qk_biased, 1)
                    item_done(dve, v_projected, n)
                    slot_free(dve, applied, n, 4)
                    dve.tensor_tensor(va[:, j, :, 0:W], ps_v[:, 0:QF].rearrange("p (h d) -> p h d", d=W),
                                      b_v[:, QF * j:QF * j + QF].rearrange("p (h d) -> p h d", d=W), ALU.add).then_inc(v_biased, 1)

                def shift(n, t, b, j, s):
                    item_done(dve, scored, n)
                    dve.tensor_reduce(st[:, s, 0, :], ps_s[:, :, 0:2, :], AX.X, ALU.max).then_inc(maxed, 1)
                    item_done(dve, maxed, n)
                    slot_free(dve, exped, n, 2)
                    dve.tensor_tensor(sx[:, s, :, :].rearrange("p (r g) j -> p r g j", g=2), ps_s[:, :, 0:2, :],
                                      st[:, s, 0, :].rearrange("p (r g) -> p r g", g=2).unsqueeze(3).to_broadcast([P, 2, 2, P]),
                                      ALU.subtract).then_inc(shifted, 1)

                def normalise(n, t, b, j, s):
                    item_done(dve, applied, n)
                    po = ps_o[:, 0:QH * (W + 1)].rearrange("p (h d) -> p h d", d=W + 1)
                    dve.reciprocal(st[:, s, 1, :], po[:, :, W]).then_inc(rowsum_inv, 1)
                    item_done(dve, rowsum_inv, n)
                    slot_free(dve, o_stored[s], n // 2, 1, 16)
                    dve.tensor_tensor(o[:, s, :, :], po[:, :, 0:W], spread(st[:, s, 1, :], W), ALU.mult).then_inc(normalised, 1)
                pipeline(dve, rounds, 2 * UNITS, [(2, per_unit8(shift)), (1, per_unit8(add_bias)), (3, per_unit8(normalise))])
        kit.clear_semaphores()


EXPERTS, FFN, TOPK = 8, 1024, 2
CAPACITY = max(1, int(1.25 * (B * S) / EXPERTS * TOPK))


def l1_moe(nc, x_in, router, w1, w2, x_out):
    with ExitStack() as stack:
        kit = Kit(nc, stack, "moe")
        acc = kit.sb("acc", [P, TILES, D])
        xt = kit.sb("xt", [P, 2, TILES, P])
        gate = kit.sb("gate", [P, EXPERTS, TILES])
        moe_route(nc, x_in, router, acc, xt, gate)
        moe_experts(nc, w1, w2, acc, xt, gate, x_out)


def moe_route(nc, x_in, router, acc, xt, gate):
    N = TILES * EXPERTS
    with ExitStack() as stack:
        kit = Kit(nc, stack, "mr")
        ident = kit.sb("ident", [P, P])
        ones = kit.sb("ones", [P, P])
        upto = kit.sb("upto", [P, P])
        rw = kit.sb("rw", [P, 2, EXPERTS])
        xcur = kit.sb("xcur", [P, 2, D])
        xtc = kit.sb("xtc", [P, 2, D])
        lg = kit.sb("lg", [P, TILES, EXPERTS])
        prio = kit.sb("prio", [P, EXPERTS])
        big = kit.sb("big", [P, 2, TILES, EXPERTS])
        eq = kit.sb("eq", [P, TILES, EXPERTS])
        hot = kit.sb("hot", [P, 2, TILES, EXPERTS])
        top = kit.sb("top", [P, 2, TILES])
        pick = kit.sb("pick", [P, TILES])
        gk = kit.sb("gk", [P, 5, TILES])
        run = [kit.sb(f"run{i}", [P, 2, TILES, EXPERTS]) for i in range(2)]
        pos = kit.sb("pos", [P, 2, TILES, EXPERTS])
        gg = kit.sb("gg", [P, 2, TILES, EXPERTS])
        ps_t = [kit.ps(f"ps_t{u}", [P, 2, P]) for u in range(2)]
        ps_l = [kit.ps(f"ps_l{u}", [P, 512]) for u in range(2)]
        ps_w = kit.ps("ps_w", [P, 2, TILES, EXPERTS])
        ps_c = kit.ps("ps_c", [P, 2, TILES, EXPERTS])
        names = ("made", "preset", "cut", "w_loaded", "transposed", "xt_copied", "xt_kept", "routed", "lg_copied",
                 "step", "exped", "counted")
        (made, preset, cut, w_loaded, transposed, xt_copied, xt_kept, routed, lg_copied,
         step, exped, counted) = (kit.sem(n) for n in names)
        x_loaded = [kit.sem(f"x_loaded{u}") for u in range(2)]
        acc_loaded = kit.sem("acc_loaded")

        with nc.Block() as block:
            @block.gpsimd
            def _(pool):
                identity_f32(nc, pool, ident, made)
                pool.memset(ones[:, :], 1.0).then_inc(preset, 1)
                pool.memset(upto[:, :], 1.0).then_inc(preset, 1)
                pool.iota(prio[:, :], pattern=[[-1, EXPERTS]], base=EXPERTS, channel_multiplier=0,
                          allow_small_or_imprecise_dtypes=True).then_inc(preset, 1)
                pool.wait_ge(preset, 3)
                pool.affine_select(out=upto[:, :], in_=upto[:, :], compare_op=ALU.is_ge, fill=0.0, base=0,
                                   pattern=[[1, P]], channel_multiplier=-1).then_inc(cut, 1)

            @block.sync
            def _(sp):
                sp.dma_start(rw[:, :, :], router.rearrange("(k p) n -> p k n", p=P)).then_inc(w_loaded, 16)
                sp.dma_start(acc[:, :, :], x_in.rearrange("t p d -> p t d")).then_inc(acc_loaded, 16)

                def load(k, u):
                    n = 2 * k + u
                    slot_free(sp, transposed, n, 2)
                    sp.dma_start(xcur[:, u, :], x_in[n, :, :]).then_inc(x_loaded[u], 16)
                pipeline(sp, TILES // 2, 2, [(0, load)])
                sp.wait_ge(acc_loaded, 16)

            @block.tensor
            def _(pe):
                pe.wait_ge(made, 2)
                pe.wait_ge(w_loaded, 16)

                def transposes(k, u):
                    n = 2 * k + u
                    item_done(pe, x_loaded[u], k, 16)
                    slot_free(pe, xt_kept, n, 2)
                    for c in range(2):
                        last = pe.transpose(ps_t[u][:, c, :], xcur[:, u, c * P:(c + 1) * P], ident[:, :])
                    last.then_inc(transposed, 1)

                def logits(k, u):
                    n = 2 * k + u
                    item_done(pe, xt_copied, n)
                    slot_free(pe, lg_copied, n, 2)
                    for c in range(2):
                        last = pe.matmul(ps_l[u][:, 0:EXPERTS], xtc[:, u, c * P:(c + 1) * P], rw[:, c, :], start=c == 0, stop=c == 1)
                    last.then_inc(routed, 1)
                pipeline(pe, TILES // 2, 2, [(0, transposes), (1, logits)])
                pe.wait_ge(cut, 1)
                pe.wait_ge(step, ONE_HOTS_DONE)
                flat = hot[:, :, :, :].rearrange("p k t e -> p (k t e)")
                pe.matmul(ps_w[:, :, :, :].rearrange("p k t e -> p (k t e)"), upto[:, :], flat, start=True, stop=True)
                pe.matmul(ps_c[:, :, :, :].rearrange("p k t e -> p (k t e)"), ones[:, :], flat, start=True, stop=True).then_inc(counted, 1)

            @block.scalar
            def _(act):
                def copy_xt(k, u):
                    n = 2 * k + u
                    item_done(act, transposed, n)
                    slot_free(act, routed, n, 2)
                    act.activation(xtc[:, u, :], ps_t[u][:, :, :].rearrange("p c t -> p (c t)"), ACT.Copy).then_inc(xt_copied, 1)
                    act.activation(xt[:, :, n, :], ps_t[u][:, :, :], ACT.Copy).then_inc(xt_kept, 1)
                pipeline(act, TILES // 2, 2, [(0, copy_xt)])
                act.wait_ge(step, DIFF_DONE)
                act.activation(gk[:, 1, :], gk[:, 0, :], ACT.Exp).then_inc(exped, 1)

            @block.vector
            def _(dve):
                def copy_logits(k, u):
                    n = 2 * k + u
                    item_done(dve, routed, n)
                    dve.tensor_scalar(lg[:, n, :], ps_l[u][:, 0:EXPERTS], 1.0, None, ALU.mult).then_inc(lg_copied, 1)
                pipeline(dve, TILES // 2, 2, [(0, copy_logits)])
                dve.wait_ge(lg_copied, TILES)
                dve.wait_ge(preset, 3)
                count = [0]

                def then(ins):
                    ins.then_inc(step, 1)
                    count[0] += 1
                    dve.wait_ge(step, count[0])

                def over_experts(a):
                    return a.unsqueeze(2).to_broadcast([P, TILES, EXPERTS])

                for c in range(2):
                    src = lg if c == 0 else big[:, 1, :, :]
                    then(dve.tensor_reduce(top[:, c, :], src[:, :, :], AX.X, ALU.max))
                    then(dve.tensor_tensor(eq[:, :, :], src[:, :, :], over_experts(top[:, c, :]), ALU.is_equal))
                    then(dve.tensor_tensor(big[:, 0, :, :], eq[:, :, :], prio[:, :].unsqueeze(1).to_broadcast([P, TILES, EXPERTS]), ALU.mult))
                    then(dve.tensor_reduce(pick[:, :], big[:, 0, :, :], AX.X, ALU.max))
                    then(dve.tensor_tensor(hot[:, c, :, :], big[:, 0, :, :], over_experts(pick[:, :]), ALU.is_equal))
                    if c == 0:
                        then(dve.scalar_tensor_tensor(out=big[:, 1, :, :], in0=hot[:, 0, :, :], scalar=-3e38, in1=lg[:, :, :],
                                                      op0=ALU.mult, op1=ALU.add))
                assert count[0] == ONE_HOTS_DONE
                then(dve.tensor_tensor(gk[:, 0, :], top[:, 1, :], top[:, 0, :], ALU.subtract))
                assert count[0] == DIFF_DONE
                dve.wait_ge(exped, 1)
                then(dve.tensor_scalar(gk[:, 2, :], gk[:, 1, :], 1.0, None, ALU.add))
                then(dve.reciprocal(gk[:, 3, :], gk[:, 2, :]))
                then(dve.tensor_tensor(gk[:, 4, :], gk[:, 1, :], gk[:, 3, :], ALU.mult))
                dve.wait_ge(counted, 1)
                then(dve.tensor_copy(run[0][:, :, :, :], ps_c[:, :, :, :]))
                shift, a = 1, 0
                while shift < TILES:
                    then(dve.tensor_copy(run[1 - a][:, :, 0:shift, :], run[a][:, :, 0:shift, :]))
                    then(dve.tensor_tensor(run[1 - a][:, :, shift:, :], run[a][:, :, shift:, :],
                                           run[a][:, :, 0:TILES - shift, :], ALU.add))
                    shift, a = 2 * shift, 1 - a
                then(dve.tensor_copy(pos[:, :, 0:1, :], ps_w[:, :, 0:1, :]))
                then(dve.tensor_tensor(pos[:, :, 1:, :], ps_w[:, :, 1:, :], run[a][:, :, 0:TILES - 1, :], ALU.add))
                then(dve.scalar_tensor_tensor(out=gg[:, :, :, :], in0=pos[:, :, :, :], scalar=float(CAPACITY), in1=hot[:, :, :, :],
                                              op0=ALU.is_le, op1=ALU.mult))
                for c in range(2):
                    then(dve.tensor_tensor(pos[:, c, :, :], gg[:, c, :, :], over_experts(gk[:, 3 + c, :]), ALU.mult))
                then(dve.tensor_tensor(gate[:, :, :].rearrange("p e t -> p t e"), pos[:, 0, :, :], pos[:, 1, :, :], ALU.add))
        kit.clear_semaphores()


ONE_HOTS_DONE = 11
DIFF_DONE = 12


def moe_experts(nc, w1, w2, acc, xt, gate, x_out):
    CT = 4
    CHUNKS, FC = TILES // CT, FFN // P
    with ExitStack() as stack:
        kit = Kit(nc, stack, "me")
        w1s = kit.sb("w1s", [P, 2, FFN])
        w2s = kit.sb("w2s", [P, FC, D])
        h = kit.sb("h", [P, 2, FC, CT * P])
        y = kit.sb("y", [P, 2, D])
        carrier = kit.sb("carrier", [P, 1])
        ps_h = [kit.ps(f"ps_h{i}", [P, CT * P]) for i in range(4)]
        ps_y = [kit.ps(f"ps_y{i}", [P, D]) for i in range(4)]
        names = ("w1_loaded", "w2_loaded", "hidden", "gelued", "down", "added", "normed")
        w1_loaded, w2_loaded, hidden, gelued, down, added, normed = (kit.sem(n) for n in names)
        stored = [kit.sem(f"stored{u}") for u in range(2)]
        norm = NormSteps(kit)

        def item(f):
            return lambda e, c: f(CHUNKS * e + c, e, c)

        with nc.Block() as block:
            @block.sync
            def _(sp):
                def load(e, c):
                    if c:
                        return
                    slot_free(sp, hidden, e, 1, CHUNKS * FC)
                    sp.dma_start(w1s[:, :, :], w1[e, :, :].rearrange("(k p) f -> p k f", p=P)).then_inc(w1_loaded, 16)
                    slot_free(sp, down, e, 1, CHUNKS * CT)
                    sp.dma_start(w2s[:, :, :], w2[e, :, :].rearrange("(k p) d -> p k d", p=P)).then_inc(w2_loaded, 16)
                pipeline(sp, EXPERTS, CHUNKS, [(0, load)])

                def store(k, u):
                    item_done(sp, normed, 2 * k + u)
                    sp.dma_start(x_out[2 * k + u, :, :], y[:, u, :]).then_inc(stored[u], 16)
                pipeline(sp, TILES // 2, 2, [(0, store)])
                for u in range(2):
                    sp.wait_ge(stored[u], 16 * TILES // 2)

            @block.tensor
            def _(pe):
                def up(n, e, c):
                    if c == 0:
                        item_done(pe, w1_loaded, e, 16)
                    for f in range(FC):
                        if f < 4:
                            slot_free(pe, gelued, FC * n + f, 4) if type(n) is int else pe.wait_ge(gelued, FC * n + f - 3)
                        else:
                            pe.wait_ge(gelued, FC * n + f - 3)
                        for kk in range(2):
                            last = pe.matmul(ps_h[f % 4][:, :], w1s[:, kk, f * P:(f + 1) * P],
                                             xt[:, kk, CT * c:CT * c + CT, :], start=kk == 0, stop=kk == 1)
                        last.then_inc(hidden, 1)

                def down_(n, e, c):
                    if c == 0:
                        item_done(pe, w2_loaded, e, 16)
                    pe.wait_ge(gelued, FC * n + FC)
                    for q in range(CT):
                        slot_free(pe, added, CT * n + q, 4)
                        for f in range(FC):
                            last = pe.matmul(ps_y[q][:, :], h[:, c % 2, f, q * P:(q + 1) * P], w2s[:, f, :],
                                             start=f == 0, stop=f == FC - 1)
                        last.then_inc(down, 1)
                pipeline(pe, EXPERTS, CHUNKS, [(0, item(up)), (1, item(down_))])

            @block.scalar
            def _(act):
                def gelu(n, e, c):
                    slot_free(act, down, CT * n + CT - 1, 2 * CT)
                    for f in range(FC):
                        act.wait_ge(hidden, FC * n + f + 1)
                        act.activation(h[:, c % 2, f, :], ps_h[f % 4][:, :], ACT.Gelu).then_inc(gelued, 1)
                pipeline(act, EXPERTS, CHUNKS, [(0, item(gelu))])

            @block.vector
            def _(dve):
                def add(e, t, q):
                    dve.wait_ge(down, TILES * e + t + 1)
                    slot_free(dve, added, TILES * e + t, TILES)
                    dve.scalar_tensor_tensor(out=acc[:, t, :], in0=ps_y[q][:, :], scalar=gate[:, e, bass.ds(t, 1)],
                                             in1=acc[:, t, :], op0=ALU.mult, op1=ALU.add).then_inc(added, 1)

                def accumulate(e, c):
                    for q in range(CT):
                        add(e, CT * c + q, q)
                pipeline(dve, EXPERTS - 1, CHUNKS, [(0, accumulate)])

                def add_last(c, q):
                    add(EXPERTS - 1, CT * c + q, q)

                def statistics(c, q):
                    t = CT * c + q
                    dve.wait_ge(added, TILES * (EXPERTS - 1) + t + 1)
                    if type(t) is not int:
                        dve.memset(carrier[:, :], 0.0)
                    norm.statistics(dve, acc[:, t, :], t, q % 2, normed)

                def apply(c, q):
                    slot_free(dve, stored[q % 2], 2 * c + q // 2, 1, 16)
                    norm.apply(dve, y[:, q % 2, :], acc[:, CT * c + q, :], CT * c + q, q % 2, normed)
                pipeline(dve, TILES // CT, CT, [(0, add_last), (1, statistics), (2, apply)], depth=6)

            @block.gpsimd
            def _(pool):
                norm.preset(pool)

                def root(k, u):
                    norm.root(pool, 2 * k + u, u, normed)
                pipeline(pool, TILES // 2, 2, [(0, root)])
        kit.clear_semaphores()


def decoder(nc, t, out):
    x1, x2, x3, x4, x5 = (nc.dram_tensor(f"x{n}", (TILES, P, D), F32, kind="Internal").ap() for n in range(1, 6))
    att0 = nc.dram_tensor("att0", (TILES, P, D), F32, kind="Internal").ap()
    l0_attn(nc, t["x"], t["wgv"], t["bgv"], att0)
    attention_output(nc, "l0ao", att0, t["wo0"], t["bo0"], t["x"], x1)
    att1 = nc.dram_tensor("att1", (TILES, P, D), F32, kind="Internal").ap()
    l0_xattn(nc, x1, t["ctx"], t["xwq"], t["xwk"], t["xwv"], t["xbq"], t["xbk"], t["xbv"], att1)
    attention_output(nc, "l0xo", att1, t["xwo"], t["xbo"], x1, x2)
    l0_ffn(nc, x2, t["fw"], t["fs"], t["fb"], x3)
    xn, mx = (nc.dram_tensor(n, (L, BM, D), F32, kind="Internal").ap() for n in ("xn", "mx"))
    toep = nc.dram_tensor("toep", (L, D, L), F32, kind="Internal").ap()
    mega_norm(nc, x3, t["mlnw"], t["mlnb"], xn)
    mega_conv(nc, xn, t["ema"], t["emag"], t["emao"], toep, mx)
    mega_attn(nc, x3, xn, mx, {k[1:]: v for k, v in t.items() if k[0] == "m"}, x4)
    att2 = nc.dram_tensor("att2", (TILES, P, 4 * D), F32, kind="Internal").ap()
    l1_xattn(nc, x4, t["ctx"], {k[1:]: v for k, v in t.items() if k[0] == "y"}, att2)
    attention_output(nc, "l1xo", att2, t["ywo"], t["ybo"], x4, x5)
    l1_moe(nc, x5, t["router"], t["w1"], t["w2"], out)


def kernel(**inputs):
    import concourse.bacc as bacc
    from concourse.bass_utils import run_bass_kernel_spmd

    def a(name):
        return np.asarray(inputs[name])

    def padded(w):
        wide = np.zeros(w.shape[:-1] + (H, 32), w.dtype)
        wide[..., :HD] = w.reshape(w.shape[:-1] + (H, HD))
        return wide.reshape(w.shape[:-1] + (H * 32,))

    arrays = {
        "x": a("x"), "ctx": a("ctx_1024"),
        "wgv": np.concatenate([a("L0_attn_Wg").T, a("L0_attn_Wv").T], axis=1),
        "bgv": np.concatenate([a("L0_attn_bg"), a("L0_attn_bv")]),
        "wo0": a("L0_attn_Wo").T, "bo0": a("L0_attn_bo"),
        "xwq": padded(a("L0_xattn_Wq").T), "xwk": padded(a("L0_xattn_Wk").T), "xwv": a("L0_xattn_Wv").T,
        "xbq": padded(a("L0_xattn_bq")).reshape(-1, P).T, "xbk": padded(a("L0_xattn_bk")).reshape(-1, P).T, "xbv": a("L0_xattn_bv"),
        "xwo": a("L0_xattn_Wo").T, "xbo": a("L0_xattn_bo"),
        "fw": a("L0_ffn_w_int8").T, "fs": a("L0_ffn_weight_scale").reshape(1), "fb": a("L0_ffn_bias"),
    }
    mw, mb = a("L1_attn_mx_w").T, a("L1_attn_mx_b")
    uh = np.r_[0:D, D + Z + HV:2 * D + Z + HV]
    half = Z // 2
    angle = np.exp(np.arange(half) * (-math.log(10000.0) / half))[:, None] * np.arange(L)[None, :]
    rot = np.stack([np.concatenate([np.cos(angle)] * 2), np.concatenate([-np.sin(angle), np.sin(angle)])], axis=1)
    same = np.where(np.arange(P)[:, None] % BQ == np.arange(P)[None, :] % BQ, 0.0, -1e30)
    ab = np.stack([a("L1_attn_rb_alpha")[0], a("L1_attn_rb_beta")[0]])
    arrays |= {
        "mlnw": a("L1_attn_ln_w"), "mlnb": a("L1_attn_ln_b"),
        "ema": np.stack([a("L1_attn_ema_" + n)[..., 0] for n in ("delta", "alpha", "beta")]),
        "emag": a("L1_attn_ema_gamma"), "emao": a("L1_attn_ema_omega").reshape(2, P).T,
        "mwv": a("L1_attn_v_w").T, "mbv": a("L1_attn_v_b"),
        "mwuh": mw[:, uh], "mbuh": mb[uh], "mwz": mw[:, D:D + Z],
        "mwr": mw[:, D + Z:D + Z + HV], "mbr": mb[D + Z:D + Z + HV],
        "mwh": a("L1_attn_h_w").T, "mbh": a("L1_attn_h_b"),
        "mzp": np.concatenate([mb[None, D:D + Z], a("L1_attn_qk_gamma"), a("L1_attn_qk_beta")]).T,
        "mrot": rot.astype(np.float32), "msame": same.astype(np.float32),
        "mab": np.stack([ab, np.roll(ab, half, axis=1)], axis=1).transpose(2, 0, 1),
    }
    bqk = np.stack([a("L1_xattn_bq"), a("L1_xattn_bk")]).reshape(2, 4, 2, P)
    arrays |= {
        "ywq": a("L1_xattn_Wq").T, "ywk": a("L1_xattn_Wk").T, "ywv": a("L1_xattn_Wv").T, "ywo": a("L1_xattn_Wo").T,
        "ybqk": bqk.transpose(3, 1, 0, 2), "ybv": a("L1_xattn_bv"), "ybo": a("L1_xattn_bo"),
        "router": a("L1_ffn_router_w").T, "w1": a("L1_ffn_w1"), "w2": a("L1_ffn_w2"),
    }
    arrays = {k: np.ascontiguousarray(v) for k, v in arrays.items()}
    nc = bacc.Bacc("TRN2", target_bir_lowering=False, num_devices=1)
    t = {k: nc.dram_tensor(f"in_{k}", v.shape, mybir.dt.from_np(v.dtype), kind="ExternalInput").ap()
         for k, v in arrays.items()}
    out = nc.dram_tensor("out_0", (B, S, D), F32, kind="ExternalOutput").ap()
    decoder(nc, t, out)
    r = run_bass_kernel_spmd(nc, [{f"in_{k}": v for k, v in arrays.items()}], core_ids=[0])
    return r.results[0]["out_0"]
```
